# Optimizing a Trainium2 kernel written in Bass

```python
import numpy as np
import jax
import jax.numpy as jnp

def _softmax(x, axis=-1):
    return jax.nn.softmax(x, axis=axis)

def _gelu(x):
    return jax.nn.gelu(x, approximate=True)

def _silu(x):
    return jax.nn.silu(x)

def _sigmoid(x):
    return jax.nn.sigmoid(x)

def _layernorm(x, axis=-1, eps=1e-05):
    m = jnp.mean(x, axis=axis, keepdims=True)
    v = jnp.var(x, axis=axis, keepdims=True)
    return (x - m) / jnp.sqrt(v + eps)

def _scatter_add(tgt, idx, src, axis=0):
    return tgt.at[idx].add(src)

def _segment_sum(src, seg, n):
    return jax.ops.segment_sum(src, seg, n)
kernel_name = 'mk_prb_d2_jaxref_r4_8b3d3a'

def setup_inputs(seed: int=0):
    np.random.seed(seed)
    _w = jnp.asarray

    def _L0_attn_setup():
        import jax, jax.numpy as jnp
        import numpy as np
        D_MODEL = 256
        N_HEADS = 16
        D_HEAD = D_MODEL // N_HEADS
        BLOCK = 128
        B, T = (2, 512)

        def _flash_attention(Q, K, V, block_size, scale):
            Bb, H, Tt, d = Q.shape
            n_blocks = Tt // block_size
            Kb = K.reshape(Bb, H, n_blocks, block_size, d).transpose(2, 0, 1, 3, 4)
            Vb = V.reshape(Bb, H, n_blocks, block_size, d).transpose(2, 0, 1, 3, 4)
            starts = jnp.arange(n_blocks) * block_size
            q_pos = jnp.arange(Tt)

            def step(carry, xs):
                m, l, acc = carry
                kb, vb, st = xs
                scores = scale * jnp.einsum('bhtd,bhsd->bhts', Q, kb)
                kv_pos = st + jnp.arange(block_size)
                future = kv_pos[None, :] > q_pos[:, None]
                scores = jnp.where(future[None, None], -jnp.inf, scores)
                m_new = jnp.maximum(m, jnp.max(scores, axis=-1, keepdims=True))
                p = jnp.exp(scores - m_new)
                corr = jnp.exp(m - m_new)
                l = corr * l + jnp.sum(p, axis=-1, keepdims=True)
                acc = corr * acc + jnp.einsum('bhts,bhsd->bhtd', p, vb)
                return ((m_new, l, acc), None)
            m0 = jnp.full((Bb, H, Tt, 1), -jnp.inf, dtype=jnp.float32)
            l0 = jnp.zeros((Bb, H, Tt, 1), dtype=jnp.float32)
            a0 = jnp.zeros((Bb, H, Tt, d), dtype=jnp.float32)
            (m, l, acc), _ = jax.lax.scan(step, (m0, l0, a0), (Kb, Vb, starts))
            return acc / jnp.maximum(l, 1e-12)
        key = jax.random.key(seed)
        ks = jax.random.split(key, 5)
        x = jax.random.normal(ks[0], (B, T, D_MODEL), dtype=jnp.float32)

        def init_w(k):
            return jax.random.normal(k, (D_MODEL, D_MODEL), dtype=jnp.float32) / np.sqrt(D_MODEL).astype(np.float32)
        return {'x': x, 'Wq': init_w(ks[1]), 'Wk': init_w(ks[2]), 'Wv': init_w(ks[3]), 'Wo': init_w(ks[4])}
    _L0_attn_in = _L0_attn_setup()

    def _L0_ffn_setup():
        import jax, jax.numpy as jnp
        import numpy as np
        D_MODEL = 256
        N_EXPERTS = 8
        TOP_K = 2
        key = jax.random.key(seed)
        ks = jax.random.split(key, 8)
        d, e = (D_MODEL, N_EXPERTS)
        s = 1.0 / np.sqrt(d)
        return {'x': jax.random.normal(ks[0], (4, 512, d), dtype=jnp.float32), 'W_gate': jax.random.uniform(ks[1], (d, e), jnp.float32, -s, s), 'b_gate': jax.random.uniform(ks[2], (e,), jnp.float32, -s, s), 'W1': jax.random.uniform(ks[3], (e, d, d), jnp.float32, -s, s), 'b1': jax.random.uniform(ks[4], (e, d), jnp.float32, -s, s), 'W2': jax.random.uniform(ks[5], (e, d, d), jnp.float32, -s, s), 'b2': jax.random.uniform(ks[6], (e, d), jnp.float32, -s, s)}
    _L0_ffn_in = _L0_ffn_setup()

    def _L1_attn_setup():
        import jax, jax.numpy as jnp
        import numpy as np
        B, N, D = (2, 512, 256)
        H = 16
        HD = D // H
        key = jax.random.key(seed)
        ks = jax.random.split(key, 5)
        scale = 1.0 / np.sqrt(D)
        return {'x': jax.random.normal(ks[0], (B, N, D), dtype=jnp.float32), 'Wq': jax.random.normal(ks[1], (D, D), dtype=jnp.float32) * scale, 'Wk': jax.random.normal(ks[2], (D, D), dtype=jnp.float32) * scale, 'Wv': jax.random.normal(ks[3], (D, D), dtype=jnp.float32) * scale, 'Wo': jax.random.normal(ks[4], (D, D), dtype=jnp.float32) * scale, 'bo': jnp.zeros((D,), dtype=jnp.float32)}
    _L1_attn_in = _L1_attn_setup()

    def _L1_ffn_setup():
        import jax, jax.numpy as jnp
        import numpy as np
        B, S, D = (4, 512, 256)
        O = 256
        E = 8
        K = 2
        key = jax.random.key(seed)
        k1, k2, k3, k4, k5 = jax.random.split(key, 5)
        scale = 1.0 / np.sqrt(D)
        x = jax.random.normal(k1, (B, S, D), dtype=jnp.float32)
        We = jax.random.uniform(k2, (E, D, O), dtype=jnp.float32, minval=-scale, maxval=scale)
        be = jax.random.uniform(k3, (E, O), dtype=jnp.float32, minval=-scale, maxval=scale)
        Wg = jax.random.uniform(k4, (D, E), dtype=jnp.float32, minval=-scale, maxval=scale)
        bg = jax.random.uniform(k5, (E,), dtype=jnp.float32, minval=-scale, maxval=scale)
        return {'x': x, 'We': We, 'be': be, 'Wg': Wg, 'bg': bg}
    _L1_ffn_in = _L1_ffn_setup()
    _d = {'L0_attn_x': _L0_attn_in['x'], 'L0_attn_Wq': _L0_attn_in['Wq'], 'L0_attn_Wk': _L0_attn_in['Wk'], 'L0_attn_Wv': _L0_attn_in['Wv'], 'L0_attn_Wo': _L0_attn_in['Wo'], 'L0_ffn_W_gate': _L0_ffn_in['W_gate'], 'L0_ffn_b_gate': _L0_ffn_in['b_gate'], 'L0_ffn_W1': _L0_ffn_in['W1'], 'L0_ffn_b1': _L0_ffn_in['b1'], 'L0_ffn_W2': _L0_ffn_in['W2'], 'L0_ffn_b2': _L0_ffn_in['b2'], 'L1_attn_Wq': _L1_attn_in['Wq'], 'L1_attn_Wk': _L1_attn_in['Wk'], 'L1_attn_Wv': _L1_attn_in['Wv'], 'L1_attn_Wo': _L1_attn_in['Wo'], 'L1_attn_bo': _L1_attn_in['bo'], 'L1_ffn_We': _L1_ffn_in['We'], 'L1_ffn_be': _L1_ffn_in['be'], 'L1_ffn_Wg': _L1_ffn_in['Wg'], 'L1_ffn_bg': _L1_ffn_in['bg']}
    _x0 = _d['L0_attn_x']
    _d['L0_attn_x'] = jax.random.normal(jax.random.fold_in(jax.random.key(seed), 1), (8, 1024, 256), dtype=_x0.dtype)
    del _x0
    return _d

def reference(L0_attn_x, L0_attn_Wq, L0_attn_Wk, L0_attn_Wv, L0_attn_Wo, L0_ffn_W_gate, L0_ffn_b_gate, L0_ffn_W1, L0_ffn_b1, L0_ffn_W2, L0_ffn_b2, L1_attn_Wq, L1_attn_Wk, L1_attn_Wv, L1_attn_Wo, L1_attn_bo, L1_ffn_We, L1_ffn_be, L1_ffn_Wg, L1_ffn_bg):

    def _L0_attn_ref(x, Wq, Wk, Wv, Wo):
        import jax, jax.numpy as jnp
        import numpy as np
        D_MODEL = 256
        N_HEADS = 16
        D_HEAD = D_MODEL // N_HEADS
        BLOCK = 128
        B, T = (2, 512)

        def _flash_attention(Q, K, V, block_size, scale):
            Bb, H, Tt, d = Q.shape
            n_blocks = Tt // block_size
            Kb = K.reshape(Bb, H, n_blocks, block_size, d).transpose(2, 0, 1, 3, 4)
            Vb = V.reshape(Bb, H, n_blocks, block_size, d).transpose(2, 0, 1, 3, 4)
            starts = jnp.arange(n_blocks) * block_size
            q_pos = jnp.arange(Tt)

            def step(carry, xs):
                m, l, acc = carry
                kb, vb, st = xs
                scores = scale * jnp.einsum('bhtd,bhsd->bhts', Q, kb)
                kv_pos = st + jnp.arange(block_size)
                future = kv_pos[None, :] > q_pos[:, None]
                scores = jnp.where(future[None, None], -jnp.inf, scores)
                m_new = jnp.maximum(m, jnp.max(scores, axis=-1, keepdims=True))
                p = jnp.exp(scores - m_new)
                corr = jnp.exp(m - m_new)
                l = corr * l + jnp.sum(p, axis=-1, keepdims=True)
                acc = corr * acc + jnp.einsum('bhts,bhsd->bhtd', p, vb)
                return ((m_new, l, acc), None)
            m0 = jnp.full((Bb, H, Tt, 1), -jnp.inf, dtype=jnp.float32)
            l0 = jnp.zeros((Bb, H, Tt, 1), dtype=jnp.float32)
            a0 = jnp.zeros((Bb, H, Tt, d), dtype=jnp.float32)
            (m, l, acc), _ = jax.lax.scan(step, (m0, l0, a0), (Kb, Vb, starts))
            return acc / jnp.maximum(l, 1e-12)
        Bx, Tx, _ = x.shape
        scale = 1.0 / np.sqrt(D_HEAD).astype(np.float32)

        def proj(W):
            y = jnp.einsum('btm,nm->btn', x, W)
            return y.reshape(Bx, Tx, N_HEADS, D_HEAD).transpose(0, 2, 1, 3)
        Q, K, V = (proj(Wq), proj(Wk), proj(Wv))
        O = _flash_attention(Q.astype(jnp.float32), K.astype(jnp.float32), V.astype(jnp.float32), BLOCK, scale)
        O = O.astype(x.dtype).transpose(0, 2, 1, 3).reshape(Bx, Tx, D_MODEL)
        return jnp.einsum('btm,nm->btn', O, Wo)

    def _L0_ffn_ref(x, W_gate, b_gate, W1, b1, W2, b2):
        import jax, jax.numpy as jnp
        import numpy as np
        D_MODEL = 256
        N_EXPERTS = 8
        TOP_K = 2
        B, T, d = x.shape
        xf = x.reshape(-1, d)
        scores = xf @ W_gate + b_gate
        topk_val, topk_idx = jax.lax.top_k(scores, TOP_K)
        onehot = jax.nn.one_hot(topk_idx, N_EXPERTS, dtype=xf.dtype)
        w = jnp.einsum('nk,nke->ne', topk_val, onehot)
        h = jax.nn.relu(jnp.einsum('nd,edh->neh', xf, W1) + b1)
        y = jnp.einsum('neh,ehd->ned', h, W2) + b2
        out = jnp.einsum('ned,ne->nd', y, w)
        return out.reshape(B, T, d)

    def _L1_attn_ref(x, Wq, Wk, Wv, Wo, bo):
        import jax, jax.numpy as jnp
        import numpy as np
        B, N, D = (2, 512, 256)
        H = 16
        HD = D // H
        b, n, _ = x.shape
        q = (x @ Wq.T).reshape(b, n, H, HD).transpose(0, 2, 1, 3)
        k = (x @ Wk.T).reshape(b, n, H, HD).transpose(0, 2, 1, 3)
        v = (x @ Wv.T).reshape(b, n, H, HD).transpose(0, 2, 1, 3)
        scores = jnp.einsum('bhqd,bhkd->bhqk', q, k) / jnp.sqrt(jnp.asarray(HD, x.dtype))
        causal = jnp.tril(jnp.ones((n, n), dtype=bool))
        scores = jnp.where(causal, scores, jnp.asarray(-jnp.inf, scores.dtype))
        probs = jax.nn.softmax(scores, axis=-1)
        out = jnp.einsum('bhqk,bhkd->bhqd', probs, v)
        out = out.transpose(0, 2, 1, 3).reshape(b, n, D)
        return out @ Wo.T + bo

    def _L1_ffn_ref(x, We, be, Wg, bg):
        import jax, jax.numpy as jnp
        import numpy as np
        B, S, D = (4, 512, 256)
        O = 256
        E = 8
        K = 2
        b, s, d = x.shape
        x_flat = x.reshape(-1, d)
        gates = jax.nn.softmax(x_flat @ Wg + bg, axis=-1)
        topk_gates, topk_idx = jax.lax.top_k(gates, K)
        topk_gates = topk_gates / jnp.sum(topk_gates, axis=1, keepdims=True)
        expert_out = jnp.einsum('nd,edo->neo', x_flat, We) + be
        selected = jnp.take_along_axis(expert_out, topk_idx[:, :, None], axis=1)
        out = jnp.sum(selected * topk_gates[:, :, None], axis=1)
        return out.reshape(b, s, -1)
    x = L0_attn_x
    xn = _layernorm(x, axis=-1)
    x = x + _L0_attn_ref(xn, L0_attn_Wq, L0_attn_Wk, L0_attn_Wv, L0_attn_Wo) + _L0_ffn_ref(xn, L0_ffn_W_gate, L0_ffn_b_gate, L0_ffn_W1, L0_ffn_b1, L0_ffn_W2, L0_ffn_b2)
    xn = _layernorm(x, axis=-1)
    x = x + _L1_attn_ref(xn, L1_attn_Wq, L1_attn_Wk, L1_attn_Wv, L1_attn_Wo, L1_attn_bo) + _L1_ffn_ref(xn, L1_ffn_We, L1_ffn_be, L1_ffn_Wg, L1_ffn_bg)
    return x

_drawn_inputs = setup_inputs


def setup_inputs(seed=0):
    import zlib

    import numpy as np

    out = dict(_drawn_inputs(seed))
    spreads = {'L1_attn_bo': (0.0, 0.1)}
    factors = {}
    for name, (base, spread) in spreads.items():
        noise = np.random.default_rng([zlib.crc32(name.encode()), seed]).standard_normal(out[name].shape)
        drawn = base * np.exp(spread * noise) if base else spread * noise
        out[name] = jnp.asarray(drawn.astype(out[name].dtype))
    for name, factor in factors.items():
        out[name] = (out[name] * factor).astype(out[name].dtype)
    return out
```

```python
from contextlib import ExitStack

import concourse.bass as bass
from concourse import mybir

F32 = mybir.dt.float32
BF16 = mybir.dt.bfloat16
ALU = mybir.AluOpType
ACT = mybir.ActivationFunctionType
AX_X = mybir.AxisListType.X

P = 128
BANK = 512
NB, T, D = 8, 1024, 256
H, DH = 16, 16
E = 8
EPS = 1e-5
TINY = 1e-12
LOWEST = -3.0e38
LAYERS = 2
NT = T // P
KD = D // P
GH = 4
NG = H // GH
HS = 32
CH = T // BANK
STACK = 6 * DH
Q_PARTS = (0, 0, 0, 1, 1, 2)
K_PARTS = (0, 1, 2, 0, 1, 0)
MROWS = 2
SROWS = STACK + MROWS

UNITS = [(g, c, k) for g in range(NG) for c in range(CH) for k in range((c + 1) * BANK // P)]
PER_G = len(UNITS) // NG
LEAD, TAIL = 10, 2
STEPS = range(-LEAD, len(UNITS) + TAIL)
PIECES = [(j, t, a, min(a + BANK, (t + 1) * P)) for j in range(GH) for t in range(NT)
          for a in range(0, (t + 1) * P, BANK)]
BUNDLES = 8
PER_BUNDLE = len(PIECES) // BUNDLES
QUANTA = CH * E * KD
MOE_LAG = 2


def bundle(s):
    g, part = (0, s + LEAD) if s < 0 else (s // PER_G + 1, s % PER_G - 2)
    if g >= NG or not 0 <= part < BUNDLES:
        return 0, []
    return g, list(range(part * PER_BUNDLE, (part + 1) * PER_BUNDLE))


def turned(s):
    g, at = (0, s + LEAD) if s < 0 else (s // PER_G + 1, s % PER_G - 2)
    return g if at == BUNDLES and g < NG else None


def due(s):
    if s < 0:
        return s + LEAD + 1
    return LEAD + min(s + 1, len(UNITS)) * (QUANTA - LEAD) // len(UNITS)


def quanta(s):
    return range(due(s - 1) if s > -LEAD else 0, due(s))


def finished(s):
    first = max(due(s - 1) - MOE_LAG, 0) if s > -LEAD else 0
    return range(first, QUANTA if s == len(UNITS) else max(due(s) - MOE_LAG, 0))


def unit_cols(u):
    _, c, k = UNITS[u]
    a = max(c * BANK, k * P)
    return a, (c + 1) * BANK - a


def is_diag(u):
    _, c, k = UNITS[u]
    return k * P >= c * BANK


def ends_chunk(u):
    return 0 <= u < len(UNITS) and UNITS[u][2] == (UNITS[u][1] + 1) * BANK // P - 1


CHUNK_OF = {u: UNITS[u][0] * CH + UNITS[u][1] for u in range(len(UNITS)) if ends_chunk(u)}
DIAG_NO = {u: n for n, u in enumerate(u for u in range(len(UNITS)) if is_diag(u))}
NDIAG = len(DIAG_NO)

MX = {}
for n in range(2 * KD * CH):
    MX["proj", n] = len(MX)
for n in range(CH):
    MX["gateT", n] = len(MX)
for s in STEPS:
    g, ps = bundle(s)
    for n in ps:
        MX["max", g, n] = len(MX)
    if turned(s) is not None:
        MX["turn", turned(s)] = len(MX)
    if ends_chunk(s - 2):
        MX["sum", CHUNK_OF[s - 2]] = len(MX)
NMX = len(MX)
ST_XT, ST_V = 0, KD * CH
ST_U = ST_V + NT
NST = ST_U + GH * len(UNITS)
assert NMX % 2 == 0 and NST % 2 == 0
NY = 2 * NT // 2
NCH = NG * CH


def attention_moe_kernel(nc, A, out):
    ctx = ExitStack()
    with ctx:
        def sb(name, shape, dt=F32):
            return ctx.enter_context(nc.sbuf_tensor(name, shape, dt))

        def sem(name):
            return ctx.enter_context(nc.semaphore(name))

        wqk = [sb(f"wqk{l}", [P, 2, KD, D]) for l in range(LAYERS)]
        wvg = [sb(f"wvg{l}", [P, KD, D + E]) for l in range(LAYERS)]
        wo = [sb(f"wo{l}", [P, NG, D]) for l in range(LAYERS)]
        bg = [sb(f"bg{l}", [P, E]) for l in range(LAYERS)]
        w1 = sb("w1", [P, E, KD, D])
        w2 = sb("w2", [P, E, KD, D])
        we = sb("we", [P, E, KD, D])
        b1 = sb("b1", [P, E, KD])
        x = sb("x", [P, NT, D])
        result = sb("result", [P, NT, D])
        xnT = sb("xnT", [P, KD, T])
        spare = sb("spare", [P, 3 * 2 * KD * T], BF16)
        parts = spare[:].rearrange("p (k q a t) -> p k q a t", k=KD, q=2, a=3)
        attn = spare[:, 0:2 * NG * T].bitcast(F32).rearrange("p (g t) -> p g t", g=NG)
        ks = sb("ks", [P, 2, GH, T], BF16)
        qs = sb("qs", [P, 2, GH, T], BF16)
        v = sb("v", [P, NT, H, HS])
        probs = sb("probs", [P, 2, GH, BANK])
        xn = probs[:].rearrange("p b h t -> p (b h t)")[:, 0:NT * D].rearrange("p (t d) -> p t d", d=D)
        late = probs[:].rearrange("p b h t -> p (b h t)")[:, NT * D:]
        rest = late[:, 0:2 * BANK].rearrange("p (b t) -> p b t", b=2)
        cgt = late[:, 2 * BANK:3 * BANK].rearrange("p (t e j) -> p t e j", e=E, j=E)
        cge = late[:, 3 * BANK:4 * BANK].rearrange("p (t e j) -> p t e j", e=E, j=E)
        oraw = sb("oraw", [P, 2, BANK])
        gateT = oraw[0:E].rearrange("p b t -> p (b t)")
        hid = sb("hid", [P, 2, BANK])
        hs = sb("hs", [P, 3, BANK])
        wb = sb("wb", [P, 4, BANK])
        mask = sb("mask", [P, BANK], BF16)
        junk = sb("junk", [P, 4])
        ident = sb("ident", [P, P])
        identb = sb("identb", [P, P], BF16)
        sel = sb("sel", [P, P])
        least4 = sb("least4", [P, GH])
        least = sb("least", [P, 1])
        stats = sb("stats", [P, NT, 6])
        mv = sb("mv", [P, NT, 2])
        rstd = sb("rstd", [P, NT])
        half = sb("half", [P, NT])
        rmax = sb("rmax", [P, GH * NT])
        rmax0 = sb("rmax0", [P, GH * NT])
        mrest = sb("mrest", [P, GH * NT])
        mparts = sb("mparts", [P, MROWS * GH * NT], BF16)
        mT = sb("mT", [MROWS * GH * NT, P], BF16)
        graw = sb("graw", [P, NT, E])
        gs = sb("gs", [P, NT, E])
        gtot = sb("gtot", [P, NT])
        ginv = sb("ginv", [P, NT])
        rank = graw
        gate = sb("gate", [P, NT, E])
        earlier = sb("earlier", [P, E, E])

        qk_dram = nc.dram_tensor("qk_parts", (KD, 2, 3, P, T), BF16, kind="Internal").ap()
        gate_dram = nc.dram_tensor("gate_rows", (E, T), F32, kind="Internal").ap()

        def bank(name):
            return ctx.enter_context(nc.psum_tensor(name, [P, BANK], F32))

        pmx = [bank(f"pmx{n}") for n in range(2)]
        pst = [bank(f"pst{n}") for n in range(2)]
        po = bank("po")
        ph = bank("ph")
        py = [bank(f"py{n}") for n in range(2)]

        w_attn = [sem(f"w_attn{l}") for l in range(LAYERS)]
        w_moe = [sem(f"w_moe{l}") for l in range(LAYERS)]
        consts = sem("consts")
        x_loaded = sem("x_loaded")
        stat_ready = sem("stat_ready")
        rstd_ready = sem("rstd_ready")
        xn_ready = sem("xn_ready")
        mx_full = sem("mx_full")
        mx_read = sem("mx_read")
        st_full = sem("st_full")
        st_read = sem("st_read")
        parts_ready = sem("parts_ready")
        qk_stored = [sem(f"qk_stored{n}") for n in range(KD)]
        qk_loaded = [sem(f"qk_loaded{n}") for n in range(2)]
        logits_ready = sem("logits_ready")
        gexp_ready = sem("gexp_ready")
        gate_ready = sem("gate_ready")
        gate_stored = sem("gate_stored")
        wb_loaded = [sem(f"wb_loaded{n}") for n in range(4)]
        msplit_ready = sem("msplit_ready")
        mrow_loaded = sem("mrow_loaded")
        masked = sem("masked")
        probs_used = sem("probs_used")
        o_read = sem("o_read")
        h_full = sem("h_full")
        h_read = sem("h_read")
        hs_ready = sem("hs_ready")
        hs_used = sem("hs_used")
        y_full = sem("y_full")
        y_read = sem("y_read")
        rows_loaded = sem("rows_loaded")
        attn_ready = sem("attn_ready")
        waits_passed = sem("waits_passed")
        stored = sem("stored")
        dve_done = sem("dve_done")
        pool_done = sem("pool_done")

        block = ctx.enter_context(nc.Block())

        def at(i, l, per_round, n):
            return i * (LAYERS * per_round) + (l * per_round + n)

        def apart(eng):
            eng.sem_inc(waits_passed, 1)

        @block.sync
        def _(sp):
            def load(dst, src, s):
                sp.dma_start(dst, src).then_inc(s, 16)

            def load_attention(l):
                load(wqk[l][:, 0], A["wk"][l].rearrange("(k p) n -> p k n", p=P), w_attn[l])
                load(wqk[l][:, 1], A["wq"][l].rearrange("(k p) n -> p k n", p=P), w_attn[l])
                load(wvg[l][:], A["wvg"][l].rearrange("(k p) n -> p k n", p=P), w_attn[l])
                load(wo[l][:], A["wo"][l].rearrange("(g p) n -> p g n", p=P), w_attn[l])
                load(bg[l][:], A["bg"][l].partition_broadcast(P), w_attn[l])

            def load_batch(i):
                sp.wait_ge(y_read, at(i, 0, NY, 2))
                apart(sp)
                sp.dma_start(x[:], A["x"][i].rearrange("(t p) d -> p t d", p=P)).then_inc(x_loaded, 16)

            def load_group(i, l, g):
                sp.wait_ge(qk_stored[g // 2], at(i, l, 32, 32))
                apart(sp)
                if g >= 2:
                    sp.wait_ge(st_read, at(i, l, NST, 2 + ST_U + GH * PER_G * (g - 1)))
                    apart(sp)
                tile, row = g // 2, (g % 2) * GH * DH
                for q, (buf, order) in enumerate(((ks, K_PARTS), (qs, Q_PARTS))):
                    src = qk_dram[tile, q, :, row:row + GH * DH, :].rearrange("a (h d) t -> a d h t", d=DH)
                    for n, a in enumerate(order):
                        sp.dma_start(buf[n * DH:(n + 1) * DH, g % 2], src[a]).then_inc(qk_loaded[g % 2], 16)

            def load_maxima(i, l, g):
                sp.wait_ge(mx_read, at(i, l, NMX, 2 + MX["turn", g] + 1))
                apart(sp)
                for a in range(MROWS):
                    row = qs[STACK + a:STACK + a + 1, g % 2].rearrange("p h (n q) -> p (h n) q", q=P)
                    sp.dma_start(row, mT[a * GH * NT:(a + 1) * GH * NT, :]).then_inc(mrow_loaded, 16)

            sp.sem_inc(stored, 1)
            load_attention(0)
            with sp.Fori(0, NB) as i:
                for l in range(LAYERS):
                    if l == 0:
                        load_batch(i)
                    sp.wait_ge(st_read, at(i, l, NST, 2))
                    apart(sp)
                    for tile in range(KD):
                        for q in range(2):
                            sp.wait_ge(parts_ready, at(i, l, 8, 2 + (tile * 2 + q + 1) * CH))
                            apart(sp)
                            sp.dma_start(qk_dram[tile, q].rearrange("a p t -> p a t"),
                                         parts[:, tile, q]).then_inc(qk_stored[tile], 16)
                        if tile == 0:
                            load_group(i, l, 0)
                    sp.wait_ge(hs_ready, at(i, l, QUANTA, 2))
                    apart(sp)
                    sp.wait_ge(mx_read, at(i, l, NMX, 2 + MX["gateT", CH - 1] + 1))
                    apart(sp)
                    sp.dma_start(gate_dram, gateT).then_inc(gate_stored, 16)
                    load_group(i, l, 1)
                    load_maxima(i, l, 0)
                    for g in range(1, NG):
                        load_maxima(i, l, g)
                        if g + 1 < NG:
                            load_group(i, l, g + 1)
                        if g == 1:
                            sp.wait_ge(attn_ready, at(i, l, NCH, CH))
                            apart(sp)
                            sp.wait_ge(gate_stored, at(i, l, 16, 16))
                            apart(sp)
                            sp.dma_start(attn[DH + 1:DH + 1 + E, 0, :], gate_dram).then_inc(rows_loaded, 16)
                    if l == LAYERS - 1:
                        sp.wait_ge(y_read, at(i, l, NY, 2 + NY))
                        apart(sp)
                        sp.dma_start(out[i].rearrange("(t p) d -> p t d", p=P), result[:]).then_inc(stored, 16)
            sp.wait_ge(stored, 1 + 16 * NB)

        @block.gpsimd
        def _(pool):
            done = [0]

            def then(ins):
                done[0] += 1
                ins.then_inc(pool_done, 1)
                pool.wait_ge(pool_done, done[0])

            pool.memset(half[:], -0.5).then_inc(parts_ready, 2)
            pool.memset(mask[:], 0.0).then_inc(hs_ready, 2)
            for m in (ident, identb, sel, v):
                then(pool.memset(m[:], 0.0))
            then(pool.memset(earlier[:], 0.0))
            pool.wait_ge(hs_ready, 2)
            for m in (ident, identb):
                then(pool.affine_select(out=m[:], in_=m[:], compare_op=ALU.not_equal, fill=1.0, base=0,
                                        pattern=[[-1, P]], channel_multiplier=1))
            then(pool.affine_select(out=sel[:].rearrange("p (j n) -> p j n", n=HS),
                                    in_=sel[:].rearrange("p (j n) -> p j n", n=HS), compare_op=ALU.not_equal,
                                    fill=1.0, base=-DH, pattern=[[-HS, GH], [0, HS]], channel_multiplier=1))
            then(pool.memset(least4[:], LOWEST))
            then(pool.affine_select(out=least4[:], in_=least4[:], compare_op=ALU.not_equal, fill=TINY, base=-DH,
                                    pattern=[[-HS, GH]], channel_multiplier=1))
            tri = mask[:, BANK - P:BANK]
            then(pool.affine_select(out=tri, in_=tri, compare_op=ALU.is_ge, fill=LOWEST, base=0,
                                    pattern=[[-1, P]], channel_multiplier=1))
            then(pool.affine_select(out=earlier[:], in_=earlier[:], compare_op=ALU.is_ge, fill=1.0, base=0,
                                    pattern=[[-1, E], [1, E]], channel_multiplier=0))
            then(pool.memset(v[:, :, :, DH:DH + 1], 1.0))
            then(pool.memset(ks[STACK:P], 1.0))
            pool.wait_ge(parts_ready, 2)
            pool.memset(mrest[:], 0.0).then_inc(consts, 1)

            base = done[0]
            per_round = [2 + CH * 2 * KD + 3 * NG, 2 + CH * 2 * KD + 3 * NG]

            with pool.Fori(0, NB) as i:
                for l in range(LAYERS):
                    count = [0]

                    def link(ins):
                        count[0] += 1
                        ins.then_inc(pool_done, 1)
                        pool.wait_ge(pool_done, at(i, l, per_round[0], base + count[0]))
                        apart(pool)

                    pool.wait_ge(stat_ready, at(i, l, 1, 1))
                    apart(pool)
                    link(pool.tensor_scalar(rstd[:], mv[:, :, 1], EPS, None, ALU.add))
                    link(pool.tensor_tensor(rstd[:], rstd[:], half[:], ALU.pow))
                    pool.tensor_copy(mrest[:, 0:1], half[:, 0:1]).then_inc(rstd_ready, 1)

                    for n in range(2 * KD * CH):
                        tile, q, c = n // (2 * CH), n // CH % 2, n % CH
                        cols = slice(c * BANK, (c + 1) * BANK)
                        pool.wait_ge(mx_read, at(i, l, NMX, 2 + MX["proj", n] + 1))
                        apart(pool)
                        link(pool.tensor_copy(parts[:, tile, q, 1, cols], rest[:, n % 2]))
                        pool.tensor_tensor(parts[:, tile, q, 2, cols], rest[:, n % 2], parts[:, tile, q, 1, cols],
                                           ALU.subtract).then_inc(parts_ready, 1)

                    def load_gate(n):
                        pool.dma_start(wb[:, n % 4], gate_dram[n % E, n // E * BANK:(n // E + 1) * BANK]
                                       .partition_broadcast(P)).then_inc(wb_loaded[n % 4], 16)

                    pool.wait_ge(gate_stored, at(i, l, 16, 16))
                    apart(pool)
                    for n in range(4):
                        load_gate(n)

                    for s in STEPS:
                        g = turned(s)
                        if g is not None:
                            pool.wait_ge(mx_read, at(i, l, NMX, 2 + MX["max", g, len(PIECES) - 1] + 1))
                            if g >= 1:
                                pool.wait_ge(mx_full, at(i, l, NMX, MX["turn", g - 1] + 1))
                            apart(pool)
                            n = GH * NT
                            link(pool.tensor_scalar(mrest[:], rmax[:], -1.0, None, ALU.mult))
                            link(pool.tensor_copy(mparts[:, 0:n], mrest[:]))
                            link(pool.tensor_tensor(mrest[:], mrest[:], mparts[:, 0:n], ALU.subtract))
                            pool.tensor_copy(mparts[:, n:2 * n], mrest[:]).then_inc(msplit_ready, 1)
                        if 0 <= s < len(UNITS) and is_diag(s):
                            pool.wait_ge(st_read, at(i, l, NST, 2 + ST_U + GH * (s + 1)))
                            apart(pool)
                            tri = probs[:, s % 2, :, 0:P]
                            pool.affine_select(out=tri, in_=tri, compare_op=ALU.is_ge, fill=0.0, base=0,
                                               pattern=[[0, GH], [1, P]], channel_multiplier=-1).then_inc(masked, 1)
                        for q in quanta(s):
                            c, e, k = q // (E * KD), q // KD % E, q % KD
                            n = c * E + e
                            pool.wait_ge(wb_loaded[n % 4], at(i, l, 64, 16 * (n // 4 + 1)))
                            pool.wait_ge(hs_used, at(i, l, QUANTA, q + 1))
                            if l == 0:
                                pool.wait_ge(h_read, i * QUANTA + (q + 2))
                                src = hid[:, q % 2]
                            else:
                                src = xnT[:, k, c * BANK:(c + 1) * BANK]
                            pool.tensor_tensor(hs[:, (l * QUANTA + q) % 3], src, wb[:, n % 4],
                                               ALU.mult).then_inc(hs_ready, 1)
                            if k == KD - 1 and n + 4 < CH * E:
                                pool.wait_ge(hs_ready, at(i, l, QUANTA, 2 + q + 1))
                                apart(pool)
                                load_gate(n + 4)
                    assert count[0] == per_round[l], count

        @block.scalar
        def _(act):
            act.wait_ge(consts, 1)
            for col, (s, n) in enumerate(((st_read, 2), (h_read, 1))):
                act.activation(graw[:, 0, col:col + 1], half[:, 0:1], ACT.Exp).then_inc(s, n)
            load = lambda dst, src, s: act.dma_start(dst, src).then_inc(s, 16)
            for dst, src in ((w1, A["w1"]), (w2, A["w2"])):
                load(dst[:], src.rearrange("e (k p) n -> p e k n", p=P), w_moe[0])
            load(b1[:], A["b1"], w_moe[0])
            load(wqk[1][:, 0], A["wk"][1].rearrange("(k p) n -> p k n", p=P), w_attn[1])
            load(wqk[1][:, 1], A["wq"][1].rearrange("(k p) n -> p k n", p=P), w_attn[1])
            load(wvg[1][:], A["wvg"][1].rearrange("(k p) n -> p k n", p=P), w_attn[1])
            load(wo[1][:], A["wo"][1].rearrange("(g p) n -> p g n", p=P), w_attn[1])
            load(bg[1][:], A["bg"][1].partition_broadcast(P), w_attn[1])
            load(we[:], A["we"].rearrange("e (k p) n -> p e k n", p=P), w_moe[1])

            with act.Fori(0, NB) as i:
                for l in range(LAYERS):
                    def full(n):
                        act.wait_ge(st_full, at(i, l, NST, n + 1))

                    for n in range(KD * CH):
                        full(ST_XT + n)
                        act.activation(xnT[:, n // CH, n % CH * BANK:(n % CH + 1) * BANK], pst[n % 2][:],
                                       ACT.Copy).then_inc(st_read, 1)
                    for t in range(NT):
                        full(ST_V + t)
                        ps = pst[(ST_V + t) % 2]
                        act.activation(v[:, t, :, 0:DH], ps[:, 0:D].rearrange("p (h d) -> p h d", d=DH), ACT.Copy)
                        act.activation(graw[:, t], ps[:, D:D + E], ACT.Copy).then_inc(st_read, 1)
                    if l == 1:
                        act.wait_ge(logits_ready, i + 1)
                        act.activation(graw[:], gs[:], ACT.Exp).then_inc(gexp_ready, 1)
                    for s in STEPS:
                        if 0 <= s < len(UNITS):
                            w = unit_cols(s)[1]
                            act.wait_ge(probs_used, at(i, l, len(UNITS), s + 1))
                            for j in range(GH):
                                n = ST_U + GH * s + j
                                full(n)
                                act.activation(probs[:, s % 2, j, 0:w], pst[n % 2][:, 0:w], ACT.Exp,
                                               scale=DH ** -0.5).then_inc(st_read, 1)
                        if l == 0:
                            for q in quanta(s):
                                act.wait_ge(h_full, i * QUANTA + (q + 1))
                                act.wait_ge(hs_ready, at(i, 0, QUANTA, q + 1))
                                act.wait_ge(w_moe[0], 48)
                                act.activation(hid[:, q % 2], ph[:], ACT.Relu,
                                               bias=b1[:, q // KD % E, q % KD:q % KD + 1]).then_inc(h_read, 1)

        @block.vector
        def _(dve):
            dve.wait_ge(consts, 1)
            dve.tensor_reduce(least[:], least4[:], AX_X, ALU.max)
            for col, (s, n) in enumerate(((mx_read, 2), (o_read, 1), (y_read, 2))):
                dve.memset(junk[:, col:col + 1], 0.0).then_inc(s, n)

            per_iter = LAYERS * (1 + 2 * KD * CH + 5) + 7

            with dve.Fori(0, NB) as i:
                count = [0]

                def link(ins):
                    count[0] += 1
                    ins.then_inc(dve_done, 1)
                    dve.wait_ge(dve_done, i * per_iter + count[0])

                for l in range(LAYERS):
                    def full(n):
                        dve.wait_ge(mx_full, at(i, l, NMX, n + 1))

                    if l == 0:
                        dve.wait_ge(x_loaded, i * 16 + 16)
                    else:
                        dve.wait_ge(y_read, at(i, 0, NY, 2 + NY))
                    for t in range(NT):
                        dve.bn_stats(stats[:, t], x[:, t])
                    for t in range(NT):
                        if t == 0:
                            link(dve.memset(junk[:, 3:4], 0.0))
                            apart(dve)
                        ins = dve.bn_aggr(mv[:, t], stats[:, t])
                    ins.then_inc(stat_ready, 1)
                    dve.wait_ge(rstd_ready, at(i, l, 1, 1))
                    for t in range(NT):
                        dve.tensor_scalar(xn[:, t], x[:, t], mv[:, t, 0:1], rstd[:, t:t + 1], ALU.subtract,
                                          ALU.mult).then_inc(xn_ready, 1)
                    for n in range(2 * KD * CH):
                        tile, q, c = n // (2 * CH), n // CH % 2, n % CH
                        cols = slice(c * BANK, (c + 1) * BANK)
                        ps = pmx[MX["proj", n] % 2]
                        full(MX["proj", n])
                        link(dve.tensor_copy(parts[:, tile, q, 0, cols], ps[:]))
                        dve.wait_ge(parts_ready, at(i, l, 8, n + 1))
                        dve.tensor_tensor(rest[:, n % 2], ps[:], parts[:, tile, q, 0, cols],
                                          ALU.subtract).then_inc(mx_read, 1)
                    dve.wait_ge(st_read, at(i, l, NST, 2 + ST_U))
                    dve.wait_ge(w_attn[l], 80)
                    tile_e = lambda a: a.unsqueeze(2).broadcast_to([P, NT, E])
                    link(dve.tensor_tensor(gs[:], graw[:], bg[l][:].unsqueeze(1).broadcast_to([P, NT, E]), ALU.add))
                    value = gs
                    if l == 1:
                        link(dve.tensor_reduce(gtot[:], gs[:], AX_X, ALU.max))
                        dve.tensor_tensor(gs[:], gs[:], tile_e(gtot[:]), ALU.subtract).then_inc(logits_ready, 1)
                        dve.wait_ge(gexp_ready, i + 1)
                        link(dve.tensor_reduce(gtot[:], graw[:], AX_X, ALU.add))
                        link(dve.reciprocal(ginv[:], gtot[:]))
                        link(dve.tensor_tensor(gs[:], graw[:], tile_e(ginv[:]), ALU.mult))
                    other = value[:].unsqueeze(2).broadcast_to([P, NT, E, E])
                    own = value[:].unsqueeze(3).broadcast_to([P, NT, E, E])
                    dve.tensor_tensor(cgt, other, own, ALU.is_gt)
                    link(dve.tensor_tensor(cge, other, own, ALU.is_ge))
                    link(dve.tensor_tensor(cge, cge, earlier[:].unsqueeze(1).broadcast_to([P, NT, E, E]),
                                           ALU.mult))
                    link(dve.tensor_tensor(cgt, cgt, cge, ALU.max))
                    link(dve.tensor_reduce(rank[:], cgt, AX_X, ALU.add))
                    pick = dve.scalar_tensor_tensor(out=gate[:], in0=rank[:], scalar=1.5, in1=value[:],
                                                    op0=ALU.is_lt, op1=ALU.mult)
                    if l == 1:
                        link(pick)
                        link(dve.tensor_reduce(gtot[:], gate[:], AX_X, ALU.add))
                        link(dve.reciprocal(ginv[:], gtot[:]))
                        pick = dve.tensor_tensor(gate[:], gate[:], tile_e(ginv[:]), ALU.mult)
                    pick.then_inc(gate_ready, 1)
                    for c in range(CH):
                        full(MX["gateT", c])
                        dve.tensor_copy(gateT[:, c * BANK:(c + 1) * BANK],
                                        pmx[MX["gateT", c] % 2][0:E, :]).then_inc(mx_read, 1)

                    for s in STEPS:
                        g, ps = bundle(s)
                        for n in ps:
                            j, t, a, b = PIECES[n]
                            col = j * NT + t
                            use = MX["max", g, n]
                            full(use)
                            src = pmx[use % 2][:, 0:b - a]
                            if b < (t + 1) * P:
                                dve.tensor_reduce(rmax0[:, col:col + 1], src, AX_X, ALU.max).then_inc(mx_read, 1)
                                dve.wait_ge(mx_read, at(i, l, NMX, 2 + use + 1))
                            else:
                                apart(dve)
                                dve.tensor_tensor_reduce(
                                    out=src, in0=src, in1=mask[:, BANK - (b - a):BANK], op0=ALU.add,
                                    op1=ALU.max, scale=1.0, scalar=rmax0[:, col:col + 1] if a else LOWEST,
                                    accum_out=rmax[:, col:col + 1]).then_inc(mx_read, 1)
                        g = turned(s)
                        if g is not None:
                            full(MX["turn", g])
                            if g >= 1:
                                dve.wait_ge(mrow_loaded, at(i, l, NG * 32, 32 * g))
                            dve.tensor_copy(mT[:], pmx[MX["turn", g] % 2][:].bitcast(BF16)[0:MROWS * GH * NT, 0:P]
                                            ).then_inc(mx_read, 1)
                        for q in finished(s):
                            if q % (E * KD) == E * KD - 1:
                                c = q // (E * KD)
                                dve.wait_ge(hs_used, at(i, l, QUANTA, 3 + q + 1))
                                for b in range(2):
                                    t = c * 4 + b * 2
                                    dve.tensor_tensor(x[:, t:t + 2].rearrange("p t d -> p (t d)"), py[b][:],
                                                      x[:, t:t + 2].rearrange("p t d -> p (t d)"),
                                                      ALU.add).then_inc(y_read, 1)
                        if ends_chunk(s - 1):
                            n = CHUNK_OF[s - 1]
                            if n == 0:
                                dve.wait_ge(gate_stored, at(i, l, 16, 16))
                            dve.wait_ge(probs_used, at(i, l, len(UNITS), 2 + s))
                            dve.tensor_scalar(oraw[:, n % 2], po[:], least[:, 0:1], None,
                                              ALU.max).then_inc(o_read, 1)
                        if ends_chunk(s - 2):
                            n = CHUNK_OF[s - 2]
                            g, c = n // CH, n % CH
                            if n == 0:
                                for stored_tile in qk_stored:
                                    dve.wait_ge(stored_tile, at(i, l, 32, 32))
                            full(MX["sum", n])
                            dst = attn[:, g, c * BANK:(c + 1) * BANK]
                            dve.reciprocal(dst, pmx[MX["sum", n] % 2][:]).then_inc(mx_read, 1)
                            dve.wait_ge(mx_read, at(i, l, NMX, 2 + MX["sum", n] + 1))
                            dve.tensor_tensor(dst, oraw[:, n % 2], dst, ALU.mult).then_inc(attn_ready, 1)
                    for b in range(NT // 2):
                        dve.wait_ge(y_full, at(i, l, NT // 2, b + 1))
                        rows = slice(2 * b, 2 * b + 2)
                        if l == 1:
                            dst = result
                            dve.wait_ge(stored, i * 16 + 1)
                        else:
                            dst = x
                        dve.tensor_tensor(dst[:, rows].rearrange("p t d -> p (t d)"), py[b % 2][:],
                                          x[:, rows].rearrange("p t d -> p (t d)"), ALU.add).then_inc(y_read, 1)
                assert count[0] == per_iter, (count, per_iter)

        @block.tensor
        def _(pe):
            pe.wait_ge(consts, 1)
            for b, (s, n) in enumerate(((probs_used, 2), (hs_used, 3))):
                pe.transpose(py[b][:, 0:P], ident[:], ident[:]).then_inc(s, n)

            with pe.Fori(0, NB) as i:
                for l in range(LAYERS):
                    pe.wait_ge(w_attn[l], 80)

                    def mx(key):
                        n = MX[key]
                        pe.wait_ge(mx_read, at(i, l, NMX, n + 1))
                        return pmx[n % 2]

                    def st(n):
                        pe.wait_ge(st_read, at(i, l, NST, n + 1))
                        return pst[n % 2]

                    pe.wait_ge(xn_ready, at(i, l, NT, NT))
                    for n in range(KD * CH):
                        k, c = n // CH, n % CH
                        ps = st(ST_XT + n)
                        for t in range(4):
                            mm = pe.transpose(ps[:, t * P:(t + 1) * P], xn[:, 4 * c + t, k * P:(k + 1) * P], ident[:])
                        mm.then_inc(st_full, 1)
                    pe.wait_ge(st_read, at(i, l, NST, 2 + ST_V))
                    for n in range(2 * KD * CH):
                        tile, q, c = n // (2 * CH), n // CH % 2, n % CH
                        ps = mx(("proj", n))
                        for k in range(KD):
                            mm = pe.matmul(ps[:], wqk[l][:, q, k, tile * P:(tile + 1) * P],
                                           xnT[:, k, c * BANK:(c + 1) * BANK], start=(k == 0), stop=(k == KD - 1))
                        mm.then_inc(mx_full, 1)
                    for t in range(NT):
                        ps = st(ST_V + t)
                        for k in range(KD):
                            mm = pe.matmul(ps[:, 0:D + E], xnT[:, k, t * P:(t + 1) * P], wvg[l][:, k],
                                           start=(k == 0), stop=(k == KD - 1))
                        mm.then_inc(st_full, 1)
                    pe.wait_ge(gate_ready, at(i, l, 1, 1))
                    for c in range(CH):
                        ps = mx(("gateT", c))
                        for t in range(4):
                            mm = pe.transpose(ps[0:E, t * P:(t + 1) * P], gate[:, 4 * c + t], ident[:])
                        mm.then_inc(mx_full, 1)

                    for s in STEPS:
                        if 0 <= s < len(UNITS):
                            g, c, kb = UNITS[s]
                            a, w = unit_cols(s)
                            pe.wait_ge(mrow_loaded, at(i, l, NG * 32, 32 * (g + 1)))
                            for j in range(GH):
                                ps = st(ST_U + GH * s + j)
                                pe.matmul(ps[:, 0:w], ks[0:SROWS, g % 2, j, kb * P:(kb + 1) * P],
                                          qs[0:SROWS, g % 2, j, a:a + w], start=True, stop=True).then_inc(st_full, 1)
                        g, ps = bundle(s)
                        for n in ps:
                            j, t, a, b = PIECES[n]
                            if n == 0:
                                pe.wait_ge(qk_loaded[g % 2], at(i, l, 2 * 12 * 16, (g // 2 + 1) * 12 * 16))
                            bk = mx(("max", g, n))
                            pe.matmul(bk[:, 0:b - a], qs[0:STACK, g % 2, j, t * P:(t + 1) * P],
                                      ks[0:STACK, g % 2, j, a:b], start=True, stop=True).then_inc(mx_full, 1)
                        g = turned(s)
                        if g is not None:
                            pe.wait_ge(msplit_ready, at(i, l, NG, g + 1))
                            bk = mx(("turn", g))
                            apart(pe)
                            pe.transpose(bk[:].bitcast(BF16)[0:MROWS * GH * NT, 0:P], mparts[:],
                                         identb[:]).then_inc(mx_full, 1)
                        if l == 0:
                            for q in quanta(s):
                                c, e, m = q // (E * KD), q // KD % E, q % KD
                                pe.wait_ge(w_moe[0], 48)
                                pe.wait_ge(h_read, i * QUANTA + (q + 1))
                                for k in range(KD):
                                    mm = pe.matmul(ph[:], w1[:, e, k, m * P:(m + 1) * P],
                                                   xnT[:, k, c * BANK:(c + 1) * BANK], start=(k == 0),
                                                   stop=(k == KD - 1))
                                mm.then_inc(h_full, 1)
                        for q in finished(s):
                            c, e, k = q // (E * KD), q // KD % E, q % KD
                            first, last = q % (E * KD) == 0, q % (E * KD) == E * KD - 1
                            pe.wait_ge(w_moe[l], 48 if l == 0 else 16)
                            pe.wait_ge(hs_ready, at(i, l, QUANTA, 2 + q + 1))
                            for t in range(4):
                                if first and t % 2 == 0:
                                    pe.wait_ge(y_read, at(i, l, NY, 2 * c + t // 2 + 1))
                                mm = pe.matmul(py[t // 2][:, t % 2 * D:(t % 2 + 1) * D],
                                               hs[:, (l * QUANTA + q) % 3, t * P:(t + 1) * P],
                                               (w2 if l == 0 else we)[:, e, k],
                                               start=first and t % 2 == 0, stop=last, skip_group_check=True)
                            mm.then_inc(hs_used, 1)
                        if 1 <= s <= len(UNITS):
                            u = s - 1
                            g, c, kb = UNITS[u]
                            a, w = unit_cols(u)
                            if is_diag(u):
                                pe.wait_ge(masked, at(i, l, NDIAG, DIAG_NO[u] + 1))
                            else:
                                pe.wait_ge(st_read, at(i, l, NST, 2 + ST_U + GH * (u + 1)))
                            if kb == 0:
                                pe.wait_ge(o_read, at(i, l, NCH, CH * g + c + 1))
                            for j in range(GH):
                                mm = pe.matmul(po[HS * j:HS * (j + 1), BANK - w:BANK], v[:, kb, GH * g + j],
                                               probs[:, u % 2, j, 0:w], start=(kb == 0), stop=ends_chunk(u))
                            mm.then_inc(probs_used, 1)
                        if ends_chunk(s - 2):
                            n = CHUNK_OF[s - 2]
                            pe.wait_ge(o_read, at(i, l, NCH, 1 + n + 1))
                            bk = mx(("sum", n))
                            pe.matmul(bk[:], sel[:], oraw[:, n % 2], start=True, stop=True).then_inc(mx_full, 1)
                    pe.wait_ge(attn_ready, at(i, l, NCH, NCH))
                    pe.wait_ge(rows_loaded, at(i, l, 16, 16))
                    for b in range(NT // 2):
                        pe.wait_ge(y_read, at(i, l, NY, 4 + b + 1))
                        for t in range(2):
                            tok = (2 * b + t) * P
                            for g in range(NG):
                                mm = pe.matmul(py[b % 2][:, t * D:(t + 1) * D], attn[:, g, tok:tok + P], wo[l][:, g],
                                               start=(t == 0 and g == 0), stop=(g == NG - 1), skip_group_check=True)
                        mm.then_inc(y_full, 1)


def kernel(**inputs):
    import numpy as np
    import concourse.bacc as bacc
    from concourse.bass_utils import run_bass_kernel_spmd

    g = {k: np.asarray(a) for k, a in inputs.items()}

    def padded(w, bias, expert_bias):
        rows = np.zeros((H, HS, D), w.dtype)
        rows[:, :DH] = w.T.reshape(H, DH, D)
        if bias is not None:
            rows[0, DH] = bias
        rows[0, DH + 1:DH + 1 + E] = expert_bias
        return rows.reshape(H * HS, D)

    per_layer = {
        "wk": [g["L0_attn_Wk"].T, g["L1_attn_Wk"].T],
        "wq": [g["L0_attn_Wq"].T, g["L1_attn_Wq"].T],
        "wvg": [np.concatenate([g["L0_attn_Wv"].T, g["L0_ffn_W_gate"]], 1),
                np.concatenate([g["L1_attn_Wv"].T, g["L1_ffn_Wg"]], 1)],
        "wo": [padded(g["L0_attn_Wo"], None, g["L0_ffn_b2"]),
               padded(g["L1_attn_Wo"], g["L1_attn_bo"], g["L1_ffn_be"])],
        "bg": [g["L0_ffn_b_gate"], g["L1_ffn_bg"]],
    }
    data = {"x": g["L0_attn_x"], "w1": g["L0_ffn_W1"], "w2": g["L0_ffn_W2"], "b1": g["L0_ffn_b1"].reshape(E, KD, P).transpose(2, 0, 1),
            "we": g["L1_ffn_We"]}
    nc = bacc.Bacc("TRN2", target_bir_lowering=False, num_devices=1)
    arrays, A = {}, {}

    def declare(name, a):
        a = np.ascontiguousarray(a)
        arrays[f"in_{name}"] = a
        return nc.dram_tensor(f"in_{name}", a.shape, mybir.dt.from_np(a.dtype), kind="ExternalInput").ap()

    for name, a in data.items():
        A[name] = declare(name, a)
    for name, both in per_layer.items():
        A[name] = [declare(f"{name}{l}", a) for l, a in enumerate(both)]
    out = nc.dram_tensor("out_0", (NB, T, D), F32, kind="ExternalOutput").ap()
    attention_moe_kernel(nc, A, out)
    r = run_bass_kernel_spmd(nc, [arrays], core_ids=[0])
    return r.results[0]["out_0"]
```

```python
from contextlib import ExitStack

import concourse.bass as bass
from concourse import mybir

F32 = mybir.dt.float32
BF16 = mybir.dt.bfloat16
ALU = mybir.AluOpType
ACT = mybir.ActivationFunctionType
AX_X = mybir.AxisListType.X

P = 128
BANK = 512
NB, T, D = 8, 1024, 256
H, DH = 16, 16
E = 8
GR = 16
EPS = 1e-5
TINY = 1e-12
LOWEST = -3.0e38
LAYERS = 2
NT = T // P
KD = D // P
GH = 4
NG = H // GH
HS = 32
CH = T // BANK
STACK = 6 * DH
Q_PARTS = (0, 0, 0, 1, 1, 2)
K_PARTS = (0, 1, 2, 0, 1, 0)
MROWS = 2
SROWS = STACK + MROWS

UNITS = [(g, c, k) for g in range(NG) for c in range(CH) for k in range((c + 1) * BANK // P)]
PER_G = len(UNITS) // NG
LEAD, TAIL = 10, 2
STEPS = range(-LEAD, len(UNITS) + TAIL)
PIECES = [(j, t, a, min(a + BANK, (t + 1) * P)) for j in range(GH) for t in range(NT)
          for a in range(0, (t + 1) * P, BANK)]
BUNDLES = 8
PER_BUNDLE = len(PIECES) // BUNDLES
QUANTA = CH * E * KD
MOE_LAG = 2


def bundle(s):
    g, part = (0, s + LEAD) if s < 0 else (s // PER_G + 1, s % PER_G - 2)
    if g >= NG or not 0 <= part < BUNDLES:
        return 0, []
    return g, list(range(part * PER_BUNDLE, (part + 1) * PER_BUNDLE))


def turned(s):
    g, at = (0, s + LEAD) if s < 0 else (s // PER_G + 1, s % PER_G - 2)
    return g if at == BUNDLES and g < NG else None


def due(s):
    if s < 0:
        return s + LEAD + 1
    return LEAD + min(s + 1, len(UNITS)) * (QUANTA - LEAD) // len(UNITS)


def quanta(s):
    return range(due(s - 1) if s > -LEAD else 0, due(s))


def finished(s):
    first = max(due(s - 1) - MOE_LAG, 0) if s > -LEAD else 0
    return range(first, QUANTA if s == len(UNITS) else max(due(s) - MOE_LAG, 0))


def unit_cols(u):
    _, c, k = UNITS[u]
    a = max(c * BANK, k * P)
    return a, (c + 1) * BANK - a


def is_diag(u):
    _, c, k = UNITS[u]
    return k * P >= c * BANK


def ends_chunk(u):
    return 0 <= u < len(UNITS) and UNITS[u][2] == (UNITS[u][1] + 1) * BANK // P - 1


CHUNK_OF = {u: UNITS[u][0] * CH + UNITS[u][1] for u in range(len(UNITS)) if ends_chunk(u)}
DIAG_NO = {u: n for n, u in enumerate(u for u in range(len(UNITS)) if is_diag(u))}
NDIAG = len(DIAG_NO)

MX = {}
for n in range(2 * KD * CH):
    MX["proj", n] = len(MX)
for n in range(CH):
    MX["gateT", n] = len(MX)
for s in STEPS:
    g, ps = bundle(s)
    for n in ps:
        MX["max", g, n] = len(MX)
    if turned(s) is not None:
        MX["turn", turned(s)] = len(MX)
    if ends_chunk(s - 2):
        MX["out", CHUNK_OF[s - 2]] = len(MX)
NMX = len(MX)
ST_XT, ST_V = 0, KD * CH
ST_U = ST_V + NT
ST_A = ST_U + GH * len(UNITS)
NST = ST_A + KD * CH
assert NMX % 2 == 0 and NST % 2 == 0
NY = 2 * NT // 2
NCH = NG * CH


def attention_moe_kernel(nc, A, out):
    ctx = ExitStack()
    with ctx:
        def sb(name, shape, dt=F32):
            return ctx.enter_context(nc.sbuf_tensor(name, shape, dt))

        def sem(name):
            return ctx.enter_context(nc.semaphore(name))

        wqk = [sb(f"wqk{l}", [P, 2, KD, D]) for l in range(LAYERS)]
        wvg = [sb(f"wvg{l}", [P, KD, D + E]) for l in range(LAYERS)]
        wo = [sb(f"wo{l}", [P, KD, D]) for l in range(LAYERS)]
        wbias = [sb(f"wbias{l}", [P, D]) for l in range(LAYERS)]
        bg = [sb(f"bg{l}", [P, E]) for l in range(LAYERS)]
        w1 = sb("w1", [P, E, KD, D])
        w2 = sb("w2", [P, E, KD, D])
        we = sb("we", [P, E, KD, D])
        b1 = sb("b1", [P, E, KD])
        x = sb("x", [P, NT, D])
        xnT = sb("xnT", [P, KD, T])
        spare = sb("spare", [P, 3 * 2 * KD * T], BF16)
        parts = spare[:].rearrange("p (k q a t) -> p k q a t", k=KD, q=2, a=3)
        attn = spare[:, 0:2 * KD * T].bitcast(F32).rearrange("p (k t) -> p k t", k=KD)
        otok = spare[:, 2 * KD * T:4 * KD * T].bitcast(F32).rearrange("p (t d) -> p t d", d=D)
        result = spare[:, 4 * KD * T:6 * KD * T].bitcast(F32).rearrange("p (t d) -> p t d", d=D)
        ks = sb("ks", [P, 2, GH, T], BF16)
        qs = sb("qs", [P, 2, GH, T], BF16)
        v = sb("v", [P, NT, H, HS])
        probs = sb("probs", [P, 2, GH, BANK])
        xn = probs[:].rearrange("p b h t -> p (b h t)")[:, 0:NT * D].rearrange("p (t d) -> p t d", d=D)
        late = probs[:].rearrange("p b h t -> p (b h t)")[:, NT * D:]
        rest = late[:, 0:2 * BANK].rearrange("p (b t) -> p b t", b=2)
        cgt = late[:, 2 * BANK:3 * BANK].rearrange("p (t e j) -> p t e j", e=E, j=E)
        cge = late[:, 3 * BANK:4 * BANK].rearrange("p (t e j) -> p t e j", e=E, j=E)
        oraw = sb("oraw", [P, 2, BANK])
        gateT = sb("gateT", [P, T])
        hid = sb("hid", [P, 2, BANK])
        hs = sb("hs", [P, 3, BANK])
        wb = sb("wb", [P, 4, BANK])
        mask = sb("mask", [P, BANK], BF16)
        junk = sb("junk", [P, 4])
        ident = sb("ident", [P, P])
        identb = sb("identb", [P, P], BF16)
        osum = sb("osum", [P, 2, BANK // P, GH])
        stats = sb("stats", [P, NT, 6])
        mv = sb("mv", [P, NT, 2])
        rstd = sb("rstd", [P, NT])
        half = sb("half", [P, NT])
        rmax = sb("rmax", [P, GH * NT])
        rmax0 = sb("rmax0", [P, GH * NT])
        mrest = sb("mrest", [P, GH * NT])
        mparts = sb("mparts", [P, MROWS * GH * NT], BF16)
        mT = sb("mT", [MROWS * GH * NT, P], BF16)
        graw = sb("graw", [P, NT, E])
        gs = sb("gs", [P, NT, E])
        gtot = sb("gtot", [P, NT])
        ginv = sb("ginv", [P, NT])
        rank = graw
        gate = sb("gate", [P, NT, GR])
        earlier = sb("earlier", [P, E, E])

        qk_dram = nc.dram_tensor("qk_parts", (KD, 2, 3, P, T), BF16, kind="Internal").ap()
        gate_dram = nc.dram_tensor("gate_rows", (E, T), F32, kind="Internal").ap()

        def bank(name):
            return ctx.enter_context(nc.psum_tensor(name, [P, BANK], F32))

        pmx = [bank(f"pmx{n}") for n in range(2)]
        pst = [bank(f"pst{n}") for n in range(2)]
        po = bank("po")
        ph = bank("ph")
        py = [bank(f"py{n}") for n in range(2)]

        w_attn = [sem(f"w_attn{l}") for l in range(LAYERS)]
        w_moe = [sem(f"w_moe{l}") for l in range(LAYERS)]
        consts = sem("consts")
        x_loaded = sem("x_loaded")
        stat_ready = sem("stat_ready")
        rstd_ready = sem("rstd_ready")
        xn_ready = sem("xn_ready")
        mx_full = sem("mx_full")
        mx_read = sem("mx_read")
        st_full = sem("st_full")
        st_read = sem("st_read")
        parts_ready = sem("parts_ready")
        qk_stored = [sem(f"qk_stored{n}") for n in range(KD)]
        qk_loaded = [sem(f"qk_loaded{n}") for n in range(2)]
        logits_ready = sem("logits_ready")
        gexp_ready = sem("gexp_ready")
        gate_ready = sem("gate_ready")
        gate_stored = sem("gate_stored")
        wb_loaded = [sem(f"wb_loaded{n}") for n in range(4)]
        msplit_ready = sem("msplit_ready")
        mrow_loaded = sem("mrow_loaded")
        masked = sem("masked")
        probs_used = sem("probs_used")
        o_read = sem("o_read")
        h_full = sem("h_full")
        h_read = sem("h_read")
        hs_ready = sem("hs_ready")
        hs_used = sem("hs_used")
        y_full = sem("y_full")
        y_read = sem("y_read")
        hi_ready = sem("hi_ready")
        mid_ready = sem("mid_ready")
        out_ready = sem("out_ready")
        waits_passed = sem("waits_passed")
        stored = sem("stored")
        dve_done = sem("dve_done")
        pool_done = sem("pool_done")

        block = ctx.enter_context(nc.Block())

        def at(i, l, per_round, n):
            return i * (LAYERS * per_round) + (l * per_round + n)

        def apart(eng):
            eng.sem_inc(waits_passed, 1)

        @block.sync
        def _(sp):
            def load(dst, src, s):
                sp.dma_start(dst, src).then_inc(s, 16)

            def load_attention(l):
                load(wqk[l][:, 0], A["wk"][l].rearrange("(k p) n -> p k n", p=P), w_attn[l])
                load(wqk[l][:, 1], A["wq"][l].rearrange("(k p) n -> p k n", p=P), w_attn[l])
                load(wvg[l][:], A["wvg"][l].rearrange("(k p) n -> p k n", p=P), w_attn[l])
                load(wo[l][:], A["wo"][l].rearrange("(k p) n -> p k n", p=P), w_attn[l])
                load(wbias[l][:], A["wbias"][l], w_attn[l])
                load(bg[l][:], A["bg"][l].partition_broadcast(P), w_attn[l])

            def load_batch(i):
                sp.wait_ge(y_read, at(i, 0, NY, 2))
                apart(sp)
                sp.dma_start(x[:], A["x"][i].rearrange("(t p) d -> p t d", p=P)).then_inc(x_loaded, 16)

            def load_group(i, l, g):
                sp.wait_ge(qk_stored[g // 2], at(i, l, 32, 32))
                apart(sp)
                if g >= 2:
                    sp.wait_ge(st_read, at(i, l, NST, 2 + ST_U + GH * PER_G * (g - 1)))
                    apart(sp)
                tile, row = g // 2, (g % 2) * GH * DH
                for q, (buf, order) in enumerate(((ks, K_PARTS), (qs, Q_PARTS))):
                    src = qk_dram[tile, q, :, row:row + GH * DH, :].rearrange("a (h d) t -> a d h t", d=DH)
                    for n, a in enumerate(order):
                        sp.dma_start(buf[n * DH:(n + 1) * DH, g % 2], src[a]).then_inc(qk_loaded[g % 2], 16)

            def load_maxima(i, l, g):
                sp.wait_ge(mx_read, at(i, l, NMX, 2 + MX["turn", g] + 1))
                apart(sp)
                for a in range(MROWS):
                    row = qs[STACK + a:STACK + a + 1, g % 2].rearrange("p h (n q) -> p (h n) q", q=P)
                    sp.dma_start(row, mT[a * GH * NT:(a + 1) * GH * NT, :]).then_inc(mrow_loaded, 16)

            sp.sem_inc(stored, 1)
            load_attention(0)
            with sp.Fori(0, NB) as i:
                for l in range(LAYERS):
                    if l == 0:
                        load_batch(i)
                    sp.wait_ge(st_read, at(i, l, NST, 2))
                    apart(sp)
                    for tile in range(KD):
                        for q in range(2):
                            sp.wait_ge(parts_ready, at(i, l, 8, 2 + (tile * 2 + q + 1) * CH))
                            apart(sp)
                            sp.dma_start(qk_dram[tile, q].rearrange("a p t -> p a t"),
                                         parts[:, tile, q]).then_inc(qk_stored[tile], 16)
                        if tile == 0:
                            load_group(i, l, 0)
                    sp.wait_ge(hs_ready, at(i, l, QUANTA, 2))
                    apart(sp)
                    sp.wait_ge(mx_read, at(i, l, NMX, 2 + MX["gateT", CH - 1] + 1))
                    apart(sp)
                    sp.dma_start(gate_dram, gateT[0:E]).then_inc(gate_stored, 16)
                    load_group(i, l, 1)
                    load_maxima(i, l, 0)
                    for g in range(1, NG):
                        load_maxima(i, l, g)
                        if g + 1 < NG:
                            load_group(i, l, g + 1)
                    if l == LAYERS - 1:
                        sp.wait_ge(y_read, at(i, l, NY, 2 + NY))
                        apart(sp)
                        sp.dma_start(out[i].rearrange("(t p) d -> p t d", p=P), result[:]).then_inc(stored, 16)
            sp.wait_ge(stored, 1 + 16 * NB)

        @block.gpsimd
        def _(pool):
            done = [0]

            def then(ins):
                done[0] += 1
                ins.then_inc(pool_done, 1)
                pool.wait_ge(pool_done, done[0])

            pool.memset(half[:], -0.5).then_inc(parts_ready, 2)
            pool.memset(mask[:], 0.0).then_inc(hs_ready, 2)
            for m in (ident, identb, v, gateT, gate):
                then(pool.memset(m[:], 0.0))
            then(pool.memset(earlier[:], 0.0))
            pool.wait_ge(hs_ready, 2)
            for m in (ident, identb):
                then(pool.affine_select(out=m[:], in_=m[:], compare_op=ALU.not_equal, fill=1.0, base=0,
                                        pattern=[[-1, P]], channel_multiplier=1))
            tri = mask[:, BANK - P:BANK]
            then(pool.affine_select(out=tri, in_=tri, compare_op=ALU.is_ge, fill=LOWEST, base=0,
                                    pattern=[[-1, P]], channel_multiplier=1))
            then(pool.affine_select(out=earlier[:], in_=earlier[:], compare_op=ALU.is_ge, fill=1.0, base=0,
                                    pattern=[[-1, E], [1, E]], channel_multiplier=0))
            then(pool.memset(v[:, :, :, DH:DH + 1], 1.0))
            then(pool.memset(ks[STACK:P], 1.0))
            then(pool.memset(gate[:, :, E:E + 1], 1.0))
            pool.wait_ge(parts_ready, 2)
            pool.memset(mrest[:], 0.0).then_inc(consts, 1)

            base = done[0]
            per_round = [2 + 3 * NG, 2 + 3 * NG]

            with pool.Fori(0, NB) as i:
                for l in range(LAYERS):
                    count = [0]

                    def link(ins):
                        count[0] += 1
                        ins.then_inc(pool_done, 1)
                        pool.wait_ge(pool_done, at(i, l, per_round[0], base + count[0]))
                        apart(pool)

                    pool.wait_ge(stat_ready, at(i, l, 1, 1))
                    apart(pool)
                    link(pool.tensor_scalar(rstd[:], mv[:, :, 1], EPS, None, ALU.add))
                    link(pool.tensor_tensor(rstd[:], rstd[:], half[:], ALU.pow))
                    pool.tensor_copy(mrest[:, 0:1], half[:, 0:1]).then_inc(rstd_ready, 1)

                    for n in range(2 * KD * CH):
                        tile, q, c = n // (2 * CH), n // CH % 2, n % CH
                        cols = slice(c * BANK, (c + 1) * BANK)
                        pool.wait_ge(mid_ready, at(i, l, 8, n + 1))
                        pool.tensor_tensor(parts[:, tile, q, 2, cols], rest[:, n % 2], parts[:, tile, q, 1, cols],
                                           ALU.subtract).then_inc(parts_ready, 1)

                    def load_gate(n):
                        pool.dma_start(wb[:, n % 4], gate_dram[n % E, n // E * BANK:(n // E + 1) * BANK]
                                       .partition_broadcast(P)).then_inc(wb_loaded[n % 4], 16)

                    pool.wait_ge(gate_stored, at(i, l, 16, 16))
                    apart(pool)
                    for n in range(4):
                        load_gate(n)

                    for s in STEPS:
                        g = turned(s)
                        if g is not None:
                            pool.wait_ge(mx_read, at(i, l, NMX, 2 + MX["max", g, len(PIECES) - 1] + 1))
                            if g >= 1:
                                pool.wait_ge(mx_full, at(i, l, NMX, MX["turn", g - 1] + 1))
                            apart(pool)
                            n = GH * NT
                            link(pool.tensor_scalar(mrest[:], rmax[:], -1.0, None, ALU.mult))
                            link(pool.tensor_copy(mparts[:, 0:n], mrest[:]))
                            link(pool.tensor_tensor(mrest[:], mrest[:], mparts[:, 0:n], ALU.subtract))
                            pool.tensor_copy(mparts[:, n:2 * n], mrest[:]).then_inc(msplit_ready, 1)
                        if 0 <= s < len(UNITS) and is_diag(s):
                            pool.wait_ge(st_read, at(i, l, NST, 2 + ST_U + GH * (s + 1)))
                            apart(pool)
                            tri = probs[:, s % 2, :, 0:P]
                            pool.affine_select(out=tri, in_=tri, compare_op=ALU.is_ge, fill=0.0, base=0,
                                               pattern=[[0, GH], [1, P]], channel_multiplier=-1).then_inc(masked, 1)
                        for q in quanta(s):
                            c, e, k = q // (E * KD), q // KD % E, q % KD
                            n = c * E + e
                            pool.wait_ge(wb_loaded[n % 4], at(i, l, 64, 16 * (n // 4 + 1)))
                            pool.wait_ge(hs_used, at(i, l, QUANTA, q + 1))
                            if l == 0:
                                pool.wait_ge(h_read, i * QUANTA + (q + 2))
                                src = hid[:, q % 2]
                            else:
                                src = xnT[:, k, c * BANK:(c + 1) * BANK]
                            pool.tensor_tensor(hs[:, (l * QUANTA + q) % 3], src, wb[:, n % 4],
                                               ALU.mult).then_inc(hs_ready, 1)
                            if k == KD - 1 and n + 4 < CH * E:
                                pool.wait_ge(hs_ready, at(i, l, QUANTA, 2 + q + 1))
                                apart(pool)
                                load_gate(n + 4)
                    assert count[0] == per_round[l], count

        @block.scalar
        def _(act):
            act.wait_ge(consts, 1)
            for col, (s, n) in enumerate(((st_read, 2), (h_read, 1), (o_read, 1))):
                act.activation(graw[:, 0, col:col + 1], half[:, 0:1], ACT.Exp).then_inc(s, n)
            load = lambda dst, src, s: act.dma_start(dst, src).then_inc(s, 16)
            for dst, src in ((w1, A["w1"]), (w2, A["w2"])):
                load(dst[:], src.rearrange("e (k p) n -> p e k n", p=P), w_moe[0])
            load(b1[:], A["b1"], w_moe[0])
            load(wqk[1][:, 0], A["wk"][1].rearrange("(k p) n -> p k n", p=P), w_attn[1])
            load(wqk[1][:, 1], A["wq"][1].rearrange("(k p) n -> p k n", p=P), w_attn[1])
            load(wvg[1][:], A["wvg"][1].rearrange("(k p) n -> p k n", p=P), w_attn[1])
            load(wo[1][:], A["wo"][1].rearrange("(k p) n -> p k n", p=P), w_attn[1])
            load(wbias[1][:], A["wbias"][1], w_attn[1])
            load(bg[1][:], A["bg"][1].partition_broadcast(P), w_attn[1])
            load(we[:], A["we"].rearrange("e (k p) n -> p e k n", p=P), w_moe[1])

            with act.Fori(0, NB) as i:
                for l in range(LAYERS):
                    def full(n):
                        act.wait_ge(st_full, at(i, l, NST, n + 1))

                    for n in range(KD * CH):
                        full(ST_XT + n)
                        act.activation(xnT[:, n // CH, n % CH * BANK:(n % CH + 1) * BANK], pst[n % 2][:],
                                       ACT.Copy).then_inc(st_read, 1)
                    for n in range(2 * KD * CH + 1):
                        if n < 2 * KD * CH:
                            tile, q, c = n // (2 * CH), n // CH % 2, n % CH
                            if l == 0 and n == 2 * CH:
                                act.wait_ge(stored, i * 16 + 1)
                            act.wait_ge(mx_full, at(i, l, NMX, MX["proj", n] + 1))
                            act.activation(parts[:, tile, q, 0, c * BANK:(c + 1) * BANK],
                                           pmx[MX["proj", n] % 2][:], ACT.Copy).then_inc(hi_ready, 1)
                        if n >= 1:
                            tile, q, c = (n - 1) // (2 * CH), (n - 1) // CH % 2, (n - 1) % CH
                            act.wait_ge(mx_read, at(i, l, NMX, 2 + MX["proj", n - 1] + 1))
                            act.activation(parts[:, tile, q, 1, c * BANK:(c + 1) * BANK], rest[:, (n - 1) % 2],
                                           ACT.Copy).then_inc(mid_ready, 1)
                    for t in range(NT):
                        full(ST_V + t)
                        ps = pst[(ST_V + t) % 2]
                        act.activation(v[:, t, :, 0:DH], ps[:, 0:D].rearrange("p (h d) -> p h d", d=DH), ACT.Copy)
                        act.activation(graw[:, t], ps[:, D:D + E], ACT.Copy).then_inc(st_read, 1)
                    if l == 1:
                        act.wait_ge(logits_ready, i + 1)
                        act.activation(graw[:], gs[:], ACT.Exp).then_inc(gexp_ready, 1)
                    for s in STEPS:
                        if 0 <= s < len(UNITS):
                            w = unit_cols(s)[1]
                            act.wait_ge(probs_used, at(i, l, len(UNITS), s + 1))
                            for j in range(GH):
                                n = ST_U + GH * s + j
                                full(n)
                                act.activation(probs[:, s % 2, j, 0:w], pst[n % 2][:, 0:w], ACT.Exp,
                                               scale=DH ** -0.5).then_inc(st_read, 1)
                        if l == 0:
                            for q in quanta(s):
                                act.wait_ge(h_full, i * QUANTA + (q + 1))
                                act.wait_ge(hs_ready, at(i, 0, QUANTA, q + 1))
                                act.wait_ge(w_moe[0], 48)
                                act.activation(hid[:, q % 2], ph[:], ACT.Relu,
                                               bias=b1[:, q // KD % E, q % KD:q % KD + 1]).then_inc(h_read, 1)
                        if ends_chunk(s - 1):
                            n = CHUNK_OF[s - 1]
                            act.wait_ge(probs_used, at(i, l, len(UNITS), 2 + s))
                            act.activation(oraw[:, n % 2], po[:], ACT.Copy).then_inc(o_read, 1)
                    for n in range(KD * CH):
                        full(ST_A + n)
                        act.activation(attn[:, n // CH, n % CH * BANK:(n % CH + 1) * BANK],
                                       pst[(ST_A + n) % 2][:], ACT.Copy).then_inc(st_read, 1)

        @block.vector
        def _(dve):
            dve.wait_ge(consts, 1)
            for col, (s, n) in enumerate(((mx_read, 2), (y_read, 2))):
                dve.memset(junk[:, col:col + 1], 0.0).then_inc(s, n)

            per_iter = LAYERS * (1 + 5 + 2 * NCH) + 7

            with dve.Fori(0, NB) as i:
                count = [0]

                def link(ins):
                    count[0] += 1
                    ins.then_inc(dve_done, 1)
                    dve.wait_ge(dve_done, i * per_iter + count[0])

                for l in range(LAYERS):
                    def full(n):
                        dve.wait_ge(mx_full, at(i, l, NMX, n + 1))

                    if l == 0:
                        dve.wait_ge(x_loaded, i * 16 + 16)
                    else:
                        dve.wait_ge(y_read, at(i, 0, NY, 2 + NY))
                    for t in range(NT):
                        dve.bn_stats(stats[:, t], x[:, t])
                    for t in range(NT):
                        if t == 0:
                            link(dve.memset(junk[:, 3:4], 0.0))
                            apart(dve)
                        ins = dve.bn_aggr(mv[:, t], stats[:, t])
                    ins.then_inc(stat_ready, 1)
                    dve.wait_ge(rstd_ready, at(i, l, 1, 1))
                    for t in range(NT):
                        dve.tensor_scalar(xn[:, t], x[:, t], mv[:, t, 0:1], rstd[:, t:t + 1], ALU.subtract,
                                          ALU.mult).then_inc(xn_ready, 1)
                    for n in range(2 * KD * CH):
                        tile, q, c = n // (2 * CH), n // CH % 2, n % CH
                        cols = slice(c * BANK, (c + 1) * BANK)
                        ps = pmx[MX["proj", n] % 2]
                        dve.wait_ge(hi_ready, at(i, l, 8, n + 1))
                        dve.wait_ge(parts_ready, at(i, l, 8, n + 1))
                        dve.tensor_tensor(rest[:, n % 2], ps[:], parts[:, tile, q, 0, cols],
                                          ALU.subtract).then_inc(mx_read, 1)
                    dve.wait_ge(st_read, at(i, l, NST, 2 + ST_U))
                    dve.wait_ge(w_attn[l], 96)
                    tile_e = lambda a: a.unsqueeze(2).broadcast_to([P, NT, E])
                    link(dve.tensor_tensor(gs[:], graw[:], bg[l][:].unsqueeze(1).broadcast_to([P, NT, E]), ALU.add))
                    value, picked = gs, gate[:, :, 0:E]
                    if l == 1:
                        link(dve.tensor_reduce(gtot[:], gs[:], AX_X, ALU.max))
                        dve.tensor_tensor(gs[:], gs[:], tile_e(gtot[:]), ALU.subtract).then_inc(logits_ready, 1)
                        dve.wait_ge(gexp_ready, i + 1)
                        link(dve.tensor_reduce(gtot[:], graw[:], AX_X, ALU.add))
                        link(dve.reciprocal(ginv[:], gtot[:]))
                        link(dve.tensor_tensor(gs[:], graw[:], tile_e(ginv[:]), ALU.mult))
                    other = value[:].unsqueeze(2).broadcast_to([P, NT, E, E])
                    own = value[:].unsqueeze(3).broadcast_to([P, NT, E, E])
                    dve.tensor_tensor(cgt, other, own, ALU.is_gt)
                    link(dve.tensor_tensor(cge, other, own, ALU.is_ge))
                    link(dve.tensor_tensor(cge, cge, earlier[:].unsqueeze(1).broadcast_to([P, NT, E, E]),
                                           ALU.mult))
                    link(dve.tensor_tensor(cgt, cgt, cge, ALU.max))
                    link(dve.tensor_reduce(rank[:], cgt, AX_X, ALU.add))
                    pick = dve.scalar_tensor_tensor(out=picked, in0=rank[:], scalar=1.5, in1=value[:],
                                                    op0=ALU.is_lt, op1=ALU.mult)
                    if l == 1:
                        link(pick)
                        link(dve.tensor_reduce(gtot[:], picked, AX_X, ALU.add))
                        link(dve.reciprocal(ginv[:], gtot[:]))
                        pick = dve.tensor_tensor(picked, picked, tile_e(ginv[:]), ALU.mult)
                    pick.then_inc(gate_ready, 1)
                    for c in range(CH):
                        full(MX["gateT", c])
                        dve.tensor_copy(gateT[0:GR, c * BANK:(c + 1) * BANK],
                                        pmx[MX["gateT", c] % 2][0:GR, :]).then_inc(mx_read, 1)

                    for s in STEPS:
                        g, ps = bundle(s)
                        for n in ps:
                            j, t, a, b = PIECES[n]
                            col = j * NT + t
                            use = MX["max", g, n]
                            full(use)
                            src = pmx[use % 2][:, 0:b - a]
                            if b < (t + 1) * P:
                                dve.tensor_reduce(rmax0[:, col:col + 1], src, AX_X, ALU.max).then_inc(mx_read, 1)
                                dve.wait_ge(mx_read, at(i, l, NMX, 2 + use + 1))
                            else:
                                apart(dve)
                                dve.tensor_tensor_reduce(
                                    out=src, in0=src, in1=mask[:, BANK - (b - a):BANK], op0=ALU.add,
                                    op1=ALU.max, scale=1.0, scalar=rmax0[:, col:col + 1] if a else LOWEST,
                                    accum_out=rmax[:, col:col + 1]).then_inc(mx_read, 1)
                        g = turned(s)
                        if g is not None:
                            full(MX["turn", g])
                            if g >= 1:
                                dve.wait_ge(mrow_loaded, at(i, l, NG * 32, 32 * g))
                            dve.tensor_copy(mT[:], pmx[MX["turn", g] % 2][:].bitcast(BF16)[0:MROWS * GH * NT, 0:P]
                                            ).then_inc(mx_read, 1)
                        for q in finished(s):
                            if q % (E * KD) == E * KD - 1:
                                c = q // (E * KD)
                                dve.wait_ge(hs_used, at(i, l, QUANTA, 3 + q + 1))
                                for b in range(2):
                                    t = c * 4 + b * 2
                                    dve.tensor_tensor(x[:, t:t + 2].rearrange("p t d -> p (t d)"), py[b][:],
                                                      x[:, t:t + 2].rearrange("p t d -> p (t d)"),
                                                      ALU.add).then_inc(y_read, 1)
                        if ends_chunk(s - 2):
                            n = CHUNK_OF[s - 2]
                            g, c = n // CH, n % CH
                            if n == 0:
                                for stored_tile in qk_stored:
                                    dve.wait_ge(stored_tile, at(i, l, 32, 32))
                            full(MX["out", n])
                            src = pmx[MX["out", n] % 2][:].rearrange("p (t h d) -> p t h d", h=GH, d=HS)
                            total = osum[:, n % 2]
                            link(dve.tensor_scalar(total, src[:, :, :, DH], TINY, None, ALU.max))
                            link(dve.reciprocal(total, total))
                            dst = otok[:, 4 * c:4 * c + 4, g * GH * DH:(g + 1) * GH * DH]
                            dve.tensor_tensor(dst.rearrange("p t (h d) -> p t h d", d=DH), src[:, :, :, 0:DH],
                                              total.unsqueeze(3).broadcast_to([P, BANK // P, GH, DH]),
                                              ALU.mult).then_inc(mx_read, 1)
                    for b in range(NT // 2):
                        dve.wait_ge(y_full, at(i, l, NT // 2, b + 1))
                        rows = slice(2 * b, 2 * b + 2)
                        if l == 1:
                            dst = result
                        else:
                            dst = x
                        dve.tensor_tensor(dst[:, rows].rearrange("p t d -> p (t d)"), py[b % 2][:],
                                          x[:, rows].rearrange("p t d -> p (t d)"), ALU.add).then_inc(y_read, 1)
                assert count[0] == per_iter, (count, per_iter)

        @block.tensor
        def _(pe):
            pe.wait_ge(consts, 1)
            for b, (s, n) in enumerate(((probs_used, 2), (hs_used, 3))):
                pe.transpose(py[b][:, 0:P], ident[:], ident[:]).then_inc(s, n)

            with pe.Fori(0, NB) as i:
                for l in range(LAYERS):
                    pe.wait_ge(w_attn[l], 96)

                    def mx(key):
                        n = MX[key]
                        pe.wait_ge(mx_read, at(i, l, NMX, n + 1))
                        return pmx[n % 2]

                    def st(n):
                        pe.wait_ge(st_read, at(i, l, NST, n + 1))
                        return pst[n % 2]

                    pe.wait_ge(xn_ready, at(i, l, NT, NT))
                    for n in range(KD * CH):
                        k, c = n // CH, n % CH
                        ps = st(ST_XT + n)
                        for t in range(4):
                            mm = pe.transpose(ps[:, t * P:(t + 1) * P], xn[:, 4 * c + t, k * P:(k + 1) * P], ident[:])
                        mm.then_inc(st_full, 1)
                    pe.wait_ge(st_read, at(i, l, NST, 2 + ST_V))
                    for n in range(2 * KD * CH):
                        tile, q, c = n // (2 * CH), n // CH % 2, n % CH
                        ps = mx(("proj", n))
                        for k in range(KD):
                            mm = pe.matmul(ps[:], wqk[l][:, q, k, tile * P:(tile + 1) * P],
                                           xnT[:, k, c * BANK:(c + 1) * BANK], start=(k == 0), stop=(k == KD - 1))
                        mm.then_inc(mx_full, 1)
                    for t in range(NT):
                        ps = st(ST_V + t)
                        for k in range(KD):
                            mm = pe.matmul(ps[:, 0:D + E], xnT[:, k, t * P:(t + 1) * P], wvg[l][:, k],
                                           start=(k == 0), stop=(k == KD - 1))
                        mm.then_inc(st_full, 1)
                    pe.wait_ge(gate_ready, at(i, l, 1, 1))
                    for c in range(CH):
                        ps = mx(("gateT", c))
                        for t in range(4):
                            mm = pe.transpose(ps[0:GR, t * P:(t + 1) * P], gate[:, 4 * c + t], ident[:])
                        mm.then_inc(mx_full, 1)

                    def scores(s, j):
                        if 0 <= s < len(UNITS):
                            g, c, kb = UNITS[s]
                            a, w = unit_cols(s)
                            if j == 0:
                                pe.wait_ge(mrow_loaded, at(i, l, NG * 32, 32 * (g + 1)))
                            ps = st(ST_U + GH * s + j)
                            pe.matmul(ps[:, 0:w], ks[0:SROWS, g % 2, j, kb * P:(kb + 1) * P],
                                      qs[0:SROWS, g % 2, j, a:a + w], start=True, stop=True).then_inc(st_full, 1)

                    def maxima(s, k):
                        g, ps = bundle(s)
                        if k < len(ps):
                            j, t, a, b = PIECES[ps[k]]
                            if ps[k] == 0:
                                pe.wait_ge(qk_loaded[g % 2], at(i, l, 2 * 12 * 16, (g // 2 + 1) * 12 * 16))
                            bk = mx(("max", g, ps[k]))
                            pe.matmul(bk[:, 0:b - a], qs[0:STACK, g % 2, j, t * P:(t + 1) * P],
                                      ks[0:STACK, g % 2, j, a:b], start=True, stop=True).then_inc(mx_full, 1)

                    def hidden(q, k):
                        if l == 0:
                            c, e, m = q // (E * KD), q // KD % E, q % KD
                            if k == 0:
                                pe.wait_ge(w_moe[0], 48)
                                pe.wait_ge(h_read, i * QUANTA + (q + 1))
                            mm = pe.matmul(ph[:], w1[:, e, k, m * P:(m + 1) * P],
                                           xnT[:, k, c * BANK:(c + 1) * BANK], start=(k == 0), stop=(k == KD - 1))
                            if k == KD - 1:
                                mm.then_inc(h_full, 1)

                    def expert_out(q, t):
                        c, e, k = q // (E * KD), q // KD % E, q % KD
                        first, last = q % (E * KD) == 0, q % (E * KD) == E * KD - 1
                        if t == 0:
                            pe.wait_ge(w_moe[l], 48 if l == 0 else 16)
                            pe.wait_ge(hs_ready, at(i, l, QUANTA, 2 + q + 1))
                        if first and t % 2 == 0:
                            pe.wait_ge(y_read, at(i, l, NY, 2 * c + t // 2 + 1))
                        mm = pe.matmul(py[t // 2][:, t % 2 * D:(t % 2 + 1) * D],
                                       hs[:, (l * QUANTA + q) % 3, t * P:(t + 1) * P],
                                       (w2 if l == 0 else we)[:, e, k],
                                       start=first and t % 2 == 0, stop=last, skip_group_check=True)
                        if t == 3:
                            mm.then_inc(hs_used, 1)

                    def attend(s):
                        if 1 <= s <= len(UNITS):
                            u = s - 1
                            g, c, kb = UNITS[u]
                            a, w = unit_cols(u)
                            if is_diag(u):
                                pe.wait_ge(masked, at(i, l, NDIAG, DIAG_NO[u] + 1))
                            else:
                                pe.wait_ge(st_read, at(i, l, NST, 2 + ST_U + GH * (u + 1)))
                            if kb == 0:
                                pe.wait_ge(o_read, at(i, l, NCH, CH * g + c + 1))
                            for j in range(GH):
                                mm = pe.matmul(po[HS * j:HS * (j + 1), BANK - w:BANK], v[:, kb, GH * g + j],
                                               probs[:, u % 2, j, 0:w], start=(kb == 0), stop=ends_chunk(u))
                            mm.then_inc(probs_used, 1)

                    for s in STEPS:
                        new, old = list(quanta(s)), list(finished(s))
                        scores(s, 0)
                        scores(s, 1)
                        maxima(s, 0)
                        attend(s)
                        maxima(s, 1)
                        scores(s, 2)
                        for q in new[:1]:
                            hidden(q, 0)
                        maxima(s, 2)
                        for q in new[:1]:
                            hidden(q, 1)
                        scores(s, 3)
                        maxima(s, 3)
                        for q in old[:1]:
                            expert_out(q, 0)
                            expert_out(q, 1)
                        maxima(s, 4)
                        for q in old[:1]:
                            expert_out(q, 2)
                            expert_out(q, 3)
                        maxima(s, 5)
                        for q in new[1:]:
                            hidden(q, 0)
                            hidden(q, 1)
                        for q in old[1:]:
                            for t in range(4):
                                expert_out(q, t)
                        g = turned(s)
                        if g is not None:
                            pe.wait_ge(msplit_ready, at(i, l, NG, g + 1))
                            bk = mx(("turn", g))
                            apart(pe)
                            pe.transpose(bk[:].bitcast(BF16)[0:MROWS * GH * NT, 0:P], mparts[:],
                                         identb[:]).then_inc(mx_full, 1)
                        if ends_chunk(s - 2):
                            n = CHUNK_OF[s - 2]
                            pe.wait_ge(o_read, at(i, l, NCH, 1 + n + 1))
                            bk = mx(("out", n))
                            for t in range(4):
                                mm = pe.transpose(bk[:, t * P:(t + 1) * P], oraw[:, n % 2, t * P:(t + 1) * P],
                                                  ident[:])
                            mm.then_inc(mx_full, 1)
                    pe.wait_ge(mx_read, at(i, l, NMX, 2 + NMX))
                    for n in range(KD * CH):
                        k, c = n // CH, n % CH
                        ps = st(ST_A + n)
                        for t in range(4):
                            mm = pe.transpose(ps[:, t * P:(t + 1) * P], otok[:, 4 * c + t, k * P:(k + 1) * P],
                                              ident[:])
                        mm.then_inc(st_full, 1)
                    pe.wait_ge(st_read, at(i, l, NST, 2 + NST))
                    for b in range(NT // 2):
                        pe.wait_ge(y_read, at(i, l, NY, 4 + b + 1))
                        for t in range(2):
                            cols = slice((2 * b + t) * P, (2 * b + t + 1) * P)
                            pe.matmul(py[b % 2][:, t * D:(t + 1) * D], gateT[:, cols], wbias[l][:],
                                      start=(t == 0), stop=False, skip_group_check=True)
                            for k in range(KD):
                                mm = pe.matmul(py[b % 2][:, t * D:(t + 1) * D], attn[:, k, cols], wo[l][:, k],
                                               start=False, stop=(k == KD - 1), skip_group_check=True)
                        mm.then_inc(y_full, 1)


def kernel(**inputs):
    import numpy as np
    import concourse.bacc as bacc
    from concourse.bass_utils import run_bass_kernel_spmd

    g = {k: np.asarray(a) for k, a in inputs.items()}

    def biases(expert_bias, out_bias):
        rows = np.zeros((P, D), expert_bias.dtype)
        rows[:E] = expert_bias
        if out_bias is not None:
            rows[E] = out_bias
        return rows

    per_layer = {
        "wk": [g["L0_attn_Wk"].T, g["L1_attn_Wk"].T],
        "wq": [g["L0_attn_Wq"].T, g["L1_attn_Wq"].T],
        "wvg": [np.concatenate([g["L0_attn_Wv"].T, g["L0_ffn_W_gate"]], 1),
                np.concatenate([g["L1_attn_Wv"].T, g["L1_ffn_Wg"]], 1)],
        "wo": [g["L0_attn_Wo"].T, g["L1_attn_Wo"].T],
        "wbias": [biases(g["L0_ffn_b2"], None), biases(g["L1_ffn_be"], g["L1_attn_bo"])],
        "bg": [g["L0_ffn_b_gate"], g["L1_ffn_bg"]],
    }
    data = {"x": g["L0_attn_x"], "w1": g["L0_ffn_W1"], "w2": g["L0_ffn_W2"], "b1": g["L0_ffn_b1"].reshape(E, KD, P).transpose(2, 0, 1),
            "we": g["L1_ffn_We"]}
    nc = bacc.Bacc("TRN2", target_bir_lowering=False, num_devices=1)
    arrays, A = {}, {}

    def declare(name, a):
        a = np.ascontiguousarray(a)
        arrays[f"in_{name}"] = a
        return nc.dram_tensor(f"in_{name}", a.shape, mybir.dt.from_np(a.dtype), kind="ExternalInput").ap()

    for name, a in data.items():
        A[name] = declare(name, a)
    for name, both in per_layer.items():
        A[name] = [declare(f"{name}{l}", a) for l, a in enumerate(both)]
    out = nc.dram_tensor("out_0", (NB, T, D), F32, kind="ExternalOutput").ap()
    attention_moe_kernel(nc, A, out)
    r = run_bass_kernel_spmd(nc, [arrays], core_ids=[0])
    return r.results[0]["out_0"]
```

```python
from contextlib import ExitStack

import concourse.bass as bass
from concourse import mybir

F32 = mybir.dt.float32
BF16 = mybir.dt.bfloat16
ALU = mybir.AluOpType
ACT = mybir.ActivationFunctionType
AX_X = mybir.AxisListType.X

P = 128
BANK = 512
NB, T, D = 8, 1024, 256
H, DH = 16, 16
E = 8
GR = 16
EPS = 1e-5
TINY = 1e-12
LOWEST = -3.0e38
LAYERS = 2
NT = T // P
KD = D // P
GH = 4
NG = H // GH
HS = 32
VW = DH + 1
VROW = H * VW + HS - VW
CH = T // BANK
STACK = 6 * DH
Q_PARTS = (0, 0, 0, 1, 1, 2)
K_PARTS = (0, 1, 2, 0, 1, 0)
MROWS = 2
SROWS = STACK + MROWS

HT = NT // CH

NSETS = CH * NG
UNITS = [(n, k) for n in range(NSETS) for k in range((n // NG + 1) * HT)]
NU = len(UNITS)
LAST = [max(u for u in range(NU) if UNITS[u][0] == n) for n in range(NSETS)]
DRAIN = 4


def pieces_of(n):
    c = n % NSETS // NG
    return [(j, t, a, min(a + BANK, (t + 1) * P)) for a in range(0, (c + 1) * BANK, BANK)
            for j in range(GH) for t in range(c * HT, (c + 1) * HT)]


NPIECES = ([0, 0, 2, 2, 3, 3, 3, 3] + [0] * 2 + [6, 6, 6, 7, 7] + [5] * 6 + [2] + [5] * 4 + [4] * 3 + [4] * 8 + [0]
           + [6] * 4 + [5] * 4 + [4] + [0])
STREAM = [(n, k) for n in range(3, NSETS + 3) for k in range(len(pieces_of(n)))]
assert len(NPIECES) == NU and sum(NPIECES) == len(STREAM)
PLACES = {0: (), 2: (0, 3), 3: (0, 2, 4), 4: (0, 2, 3, 5), 5: (0, 2, 3, 4, 5), 6: (0, 1, 2, 3, 4, 5),
          7: (0, 1, 2, 3, 4, 5, 6)}
TURNS = {}
for n in range(3, NSETS + 3):
    end = sum(1 for m, _ in STREAM if m <= n)
    s = next(s for s in range(NU) if sum(NPIECES[:s + 1]) >= end) + 1
    TURNS[s + {3: 1, 8: 1}.get(n, 0)] = n

QUANTA = CH * E * KD
LAG = 3
NHALVES = 2 * QUANTA + LAG
CHUNK_HALVES = QUANTA + LAG
X_FULL = 25


def spread(first, last, count, light):
    n = [1 if s in light else 0 for s in range(first, last + 1)]
    rest, free = count - sum(n), [k for k, a in enumerate(n) if a == 0]
    for m, k in enumerate(free):
        n[k] = (m + 1) * rest // len(free) - m * rest // len(free)
    return n


HALVES = ([0] * 4 + spread(4, X_FULL, CHUNK_HALVES, (4, 5, 6, 7, 10, 11, X_FULL))
          + spread(X_FULL + 1, NU + 2, NHALVES - CHUNK_HALVES, (32, 33, 34, 35, 45)))
assert len(HALVES) == NU + 3 and sum(HALVES) == NHALVES and max(HALVES) <= 2

OT0, Y0 = LAST[NG - 1] + 3, X_FULL + 2
LN0, XT0, PROJ0, V0 = Y0 + 2, Y0 + 4, (32, 33, 34, 35), (45, 45, 46, 47)
GATES, GATE_ROWS = (0, 16), (2, 20)
GATE_PARTS, GATE_PACE = 13, (2, 1)
LN1, XT1, PROJ1, V1 = 3, 5, (6, 6, 7, 7), (8, 9, 10, 11)
OT1, Y1 = LAST[NSETS - 1] + 3, LAST[NSETS - 1] + 4
WB_FIRST = (4, 21)
NP = 2 * KD


def now(l, s):
    return [(0, NU + s), (1, s)] if l == 1 and s < DRAIN else [(l, s)]


def unit(l, s):
    return s if l >= 0 and 0 <= s < NU else None


def bundle(l, s):
    if not 0 <= s < NU:
        return []
    a = sum(NPIECES[:s])
    return [(n, k) for n, k in STREAM[a:a + NPIECES[s]] if l >= 0 or n >= NSETS]


def attends_late(l, s):
    return not halves(l, s)


def before_turn(l, s):
    n = len(bundle(l, s))
    return sum(1 for place in PLACES[n] if place <= (2 if attends_late(l, s) else 1))


def turned(l, s):
    n = TURNS.get(s)
    return n if n is not None and (l >= 0 or n >= NSETS) else None


def halves(l, s):
    return [(r, sum(HALVES[:d]) + m) for r, d in now(l, s) if r >= 0 and 0 <= d < len(HALVES)
            for m in range(HALVES[d])]


def begun(l, s):
    return [(r, p // 2) for r, p in halves(l, s) if p % 2 == 1 and p < 2 * QUANTA]


def experts_done(l, s):
    return [(r, (p - LAG) // QUANTA) for r, p in halves(l, s) if p >= LAG and (p - LAG + 1) % QUANTA == 0]


def ends_set(s):
    return LAST.index(s) if s in LAST else None


def projections(l, s):
    return ([(1, n, l) for n, at_step in enumerate(PROJ1) if at_step == s and l >= 0]
            + [(0, n, l + 1) for n, at_step in enumerate(PROJ0) if at_step == s])


def value_tiles(l, s):
    return ([(HT + n, l) for n, at_step in enumerate(V1) if at_step == s and l >= 0]
            + [(n, l + 1) for n, at_step in enumerate(V0) if at_step == s])


def unit_cols(u):
    n, k = UNITS[u]
    c = n // NG
    a = max(c * BANK, k * P)
    return a, (c + 1) * BANK - a


def is_diag(u):
    n, k = UNITS[u]
    return k >= n // NG * HT


DIAG_NO = {u: n for n, u in enumerate(u for u in range(NU) if is_diag(u))}
NDIAG = len(DIAG_NO)

BEFORE = [(-1, s) for s in range(LN0, NU)]
BODY = [(l, s) for l in range(LAYERS) for s in range(NU + (DRAIN if l == LAYERS - 1 else 0))]


def uses():
    mx, st, begin = {}, {}, {}
    for part in (BEFORE, BODY):
        for l, s in part:
            if s == 0:
                begin[l] = (len(mx), len(st))
            for n, k in bundle(l, s)[:before_turn(l, s)]:
                mx[l, "max", n, k] = len(mx)
            if turned(l, s) is not None:
                mx[l, "turn", turned(l, s)] = len(mx)
            for n, k in bundle(l, s)[before_turn(l, s):]:
                mx[l, "max", n, k] = len(mx)
            if unit(l, s) is not None:
                for j in range(GH):
                    st[l, "unit", s, j] = len(st)
            for r, d in now(l, s):
                if r >= 0 and ends_set(d - 2) is not None:
                    mx[r, "out", ends_set(d - 2)] = len(mx)
                for c, at_step in enumerate((OT0, OT1)):
                    if r >= 0 and d == at_step:
                        for k in range(KD):
                            st[r, "oT", c, k] = len(st)
                for c, at_step in enumerate((Y0, Y1)):
                    if r >= 0 and d == at_step:
                        for b in range(2 * c, 2 * c + 2):
                            mx[r, "y", b] = len(mx)
                if r >= 0 and d in GATE_ROWS:
                    mx[r, "gateT", GATE_ROWS.index(d)] = len(mx)
                for c, at_step in enumerate((XT0, XT1)):
                    if d == at_step and (r >= 0 or c == 0):
                        for k in range(KD):
                            st[r, "xT", c, k] = len(st)
                for c, n, _ in projections(r, d):
                    mx[r, "proj", c, n] = len(mx)
                for t, _ in value_tiles(r, d):
                    st[r, "v", t] = len(st)
    return mx, st, begin


MX, ST, BEGIN = uses()
LOOP_MX, LOOP_ST = BEGIN[0]
NMX, NST = len(MX) - LOOP_MX, len(ST) - LOOP_ST
assert NMX % 2 == NST % 2 == 0
NY = 2 * CH


def attention_moe_kernel(nc, A, out):
    ctx = ExitStack()
    with ctx:
        def sb(name, shape, dt=F32):
            return ctx.enter_context(nc.sbuf_tensor(name, shape, dt))

        def sem(name):
            return ctx.enter_context(nc.semaphore(name))

        wqk = [sb(f"wqk{l}", [P, 2, KD, D]) for l in range(LAYERS)]
        wvg = [sb(f"wvg{l}", [P, KD, D + E]) for l in range(LAYERS)]
        wo = [sb(f"wo{l}", [P, KD, D]) for l in range(LAYERS)]
        wbias = [sb(f"wbias{l}", [P, D]) for l in range(LAYERS)]
        bg = [sb(f"bg{l}", [P, E]) for l in range(LAYERS)]
        w1 = sb("w1", [P, E, KD, D])
        w2 = sb("w2", [P, E, KD, D])
        we = sb("we", [P, E, KD, D])
        b1 = sb("b1", [P, E, KD])
        x = sb("x", [P, NT, D])
        xnT = sb("xnT", [P, KD, T])
        xn = sb("xn", [P, HT, D])
        parts = sb("parts", [P, KD, 2, 3, BANK], BF16)
        rest = sb("rest", [P, 2, BANK])
        k_first = sb("k_first", [P, NG, GH, BANK], BF16)
        k_second = sb("k_second", [P, 2, GH, BANK], BF16)
        qs = sb("qs", [P, NG, GH, BANK], BF16)
        v = sb("v", [P, NT, VROW])
        probs = sb("probs", [P, 2, GH, BANK])
        oraw = sb("oraw", [P, BANK])
        otok = sb("otok", [P, HT, D])
        turned_out = sb("turned_out", [P, HT * D])
        attn = turned_out[:].rearrange("p (k t) -> p k t", k=KD)
        result = turned_out[:].rearrange("p (t d) -> p t d", d=D)
        gateT = sb("gateT", [P, T])
        hid = sb("hid", [P, 2, BANK])
        hs = sb("hs", [P, 3, BANK])
        wb = sb("wb", [P, 4, BANK])
        mask = sb("mask", [P, BANK], BF16)
        junk = sb("junk", [P, 4])
        ident = sb("ident", [P, P])
        identb = sb("identb", [P, P], BF16)
        osum = sb("osum", [P, 2, HT, GH])
        stats = sb("stats", [P, NT, 6])
        mv = sb("mv", [P, NT, 2])
        rstd = sb("rstd", [P, NT])
        half = sb("half", [P, NT])
        rmax = sb("rmax", [P, 2, GH * HT])
        rmax0 = sb("rmax0", [P, GH * HT])
        mrest = sb("mrest", [P, GH * HT])
        mparts = sb("mparts", [P, MROWS * GH * HT], BF16)
        mT = sb("mT", [MROWS * GH * HT, P], BF16)
        graw = sb("graw", [P, NT, E])
        gs = sb("gs", [P, NT, E])
        gtot = sb("gtot", [P, NT])
        ginv = sb("ginv", [P, NT])
        rank = graw
        gate = sb("gate", [P, NT, GR])
        cgt = sb("cgt", [P, HT, E, E])
        cge = sb("cge", [P, HT, E, E])
        earlier = sb("earlier", [P, E, E])

        qk_dram = nc.dram_tensor("qk_parts", (CH, KD, 2, 3, P, BANK), BF16, kind="Internal").ap()
        gate_dram = nc.dram_tensor("gate_rows", (CH, E, BANK), F32, kind="Internal").ap()

        def bank(name):
            return ctx.enter_context(nc.psum_tensor(name, [P, BANK], F32))

        pmx = [bank(f"pmx{n}") for n in range(2)]
        pst = [bank(f"pst{n}") for n in range(2)]
        po = bank("po")
        ph = bank("ph")
        py = [bank(f"py{n}") for n in range(2)]

        w_attn = [sem(f"w_attn{l}") for l in range(LAYERS)]
        w_moe = [sem(f"w_moe{l}") for l in range(LAYERS)]
        consts = sem("consts")
        x_loaded = [sem(f"x_loaded{c}") for c in range(CH)]
        stat_ready = sem("stat_ready")
        rstd_ready = sem("rstd_ready")
        xn_ready = sem("xn_ready")
        mx_full = sem("mx_full")
        mx_read = sem("mx_read")
        st_full = sem("st_full")
        st_read = sem("st_read")
        parts_ready = sem("parts_ready")
        qk_stored = [sem(f"qk_stored{n}") for n in range(KD)]
        q_loaded = [sem(f"q_loaded{n}") for n in range(NG)]
        k_first_loaded = [sem(f"k_first_loaded{n}") for n in range(NG)]
        k_second_loaded = [sem(f"k_second_loaded{n}") for n in range(2)]
        logits_ready = sem("logits_ready")
        gexp_ready = sem("gexp_ready")
        gate_ready = sem("gate_ready")
        gate_stored = [sem(f"gate_stored{c}") for c in range(CH)]
        wb_loaded = [sem(f"wb_loaded{n}") for n in range(4)]
        msplit_ready = sem("msplit_ready")
        mrow_loaded = sem("mrow_loaded")
        masked = sem("masked")
        probs_used = sem("probs_used")
        o_read = sem("o_read")
        h_full = sem("h_full")
        h_read = sem("h_read")
        hs_ready = sem("hs_ready")
        hs_used = sem("hs_used")
        y_read = sem("y_read")
        hi_ready = sem("hi_ready")
        mid_ready = sem("mid_ready")
        waits_passed = sem("waits_passed")
        stored = [sem(f"stored{c}") for c in range(CH)]
        dve_done = sem("dve_done")
        pool_done = sem("pool_done")

        block = ctx.enter_context(nc.Block())

        def at(i, l, per_round, n):
            return i * (LAYERS * per_round) + (l * per_round + n)

        def apart(eng):
            eng.sem_inc(waits_passed, 1)

        def mx_no(i, *key):
            return i * NMX + MX[key]

        def st_no(i, *key):
            return i * NST + ST[key]

        def mx_done(i, *key):
            return mx_no(i, *key) + 3

        def st_done(i, *key):
            return st_no(i, *key) + 3

        def own_chain(eng, s, per_iter):
            count, before = [0], [0]

            def link(i, ins):
                count[0] += 1
                ins.then_inc(s, 1)
                eng.wait_ge(s, i * per_iter + (before[0] + count[0]))
                apart(eng)

            def enter_loop():
                before[0], count[0] = count[0], 0

            def leave_loop():
                assert count[0] == per_iter, (count, per_iter)
            return link, enter_loop, leave_loop

        @block.sync
        def _(sp):
            def load(dst, src, s):
                sp.dma_start(dst, src).then_inc(s, 16)

            def load_attention(l):
                load(wqk[l][:, 0], A["wk"][l].rearrange("(k p) n -> p k n", p=P), w_attn[l])
                load(wqk[l][:, 1], A["wq"][l].rearrange("(k p) n -> p k n", p=P), w_attn[l])
                load(wvg[l][:], A["wvg"][l].rearrange("(k p) n -> p k n", p=P), w_attn[l])
                load(wo[l][:], A["wo"][l].rearrange("(k p) n -> p k n", p=P), w_attn[l])
                load(wbias[l][:], A["wbias"][l], w_attn[l])
                load(bg[l][:], A["bg"][l].partition_broadcast(P), w_attn[l])

            def load_x(b, c):
                sp.dma_start(x[:, c * HT:(c + 1) * HT],
                             A["x"][b].rearrange("(c t p) d -> c p t d", p=P, c=CH)[c]).then_inc(x_loaded[c], 16)

            def store_result(i, c):
                sp.dma_start(out[i].rearrange("(c t p) d -> c p t d", p=P, c=CH)[c], result).then_inc(stored[c], 16)

            def store_parts(i, l, c, tile):
                for q in range(2):
                    sp.wait_ge(parts_ready, at(i, l, CH * NP, 2 + c * NP + tile * 2 + q + 1))
                    apart(sp)
                    sp.dma_start(qk_dram[c, tile, q].rearrange("a p t -> p a t"),
                                 parts[:, tile, q]).then_inc(qk_stored[tile], 16)

            def load_stack(i, l, n, q, buf, s):
                c, g = n // NG, n % NG
                sp.wait_ge(qk_stored[g // 2], at(i, l, CH * 32, (c + 1) * 32))
                apart(sp)
                row = (g % 2) * GH * DH
                src = qk_dram[c, g // 2, q, :, row:row + GH * DH, :].rearrange("a (h d) t -> a d h t", d=DH)
                for m, a in enumerate((K_PARTS, Q_PARTS)[q]):
                    sp.dma_start(buf[m * DH:(m + 1) * DH], src[a]).then_inc(s, 16)

            def scores_done(i, l, n):
                sp.wait_ge(st_read, st_done(i, l, "unit", LAST[n], GH - 1))
                apart(sp)

            def load_q(i, l, n):
                load_stack(i, l, n, 1, qs[:, n % NG], q_loaded[n % NG])

            def load_k(i, l, n):
                if n < NG:
                    load_stack(i, l, n, 0, k_first[:, n], k_first_loaded[n])
                else:
                    load_stack(i, l, n, 0, k_second[:, n % 2], k_second_loaded[n % 2])

            def load_maxima(i, l, n):
                sp.wait_ge(mx_read, mx_done(i, l, "turn", n))
                apart(sp)
                for a in range(MROWS):
                    row = qs[STACK + a:STACK + a + 1, n % NG].rearrange("p h (n q) -> p (h n) q", q=P)
                    sp.dma_start(row, mT[a * GH * HT:(a + 1) * GH * HT, :]).then_inc(mrow_loaded, 16)

            def store_gates(i, l, c):
                sp.wait_ge(hs_ready, at(i, l, QUANTA, 2))
                apart(sp)
                sp.wait_ge(mx_read, mx_done(i, l, "gateT", c))
                apart(sp)
                sp.dma_start(gate_dram[c], gateT[0:E, c * BANK:(c + 1) * BANK]).then_inc(gate_stored[c], 16)

            def next_batch(i, c):
                sp.wait_ge(mx_read, mx_done(i, LAYERS - 1, "y", 2 * c + 1))
                apart(sp)
                load_x((i + 1) % NB, c)
                store_result(i, c)

            for c in range(CH):
                sp.sem_inc(stored[c], 1)
                load_x(0, c)
            load_attention(0)
            for n in range(NG):
                if n % 2 == 0:
                    store_parts(0, 0, 0, n // 2)
                load_q(0, 0, n)
                load_k(0, 0, n)
            for n in range(3):
                load_maxima(0, -1, NSETS + n)
            with sp.Fori(0, NB) as i:
                for l in range(LAYERS):
                    store_gates(i, l, 0)
                    store_parts(i, l, 1, 0)
                    scores_done(i, l, 0)
                    load_q(i, l, 4)
                    load_k(i, l, 4)
                    store_parts(i, l, 1, 1)
                    scores_done(i, l, 1)
                    load_q(i, l, 5)
                    load_k(i, l, 5)
                    load_maxima(i, l, 3)
                    scores_done(i, l, 2)
                    load_q(i, l, 6)
                    load_maxima(i, l, 4)
                    scores_done(i, l, 3)
                    load_q(i, l, 7)
                    store_gates(i, l, 1)
                    load_maxima(i, l, 5)
                    scores_done(i, l, 4)
                    load_k(i, l, 6)
                    if l == LAYERS - 1:
                        next_batch(i, 0)
                    load_maxima(i, l, 6)
                    scores_done(i, l, 5)
                    load_k(i, l, 7)
                    store_parts(i, l + 1, 0, 0)
                    for n in range(2):
                        load_q(i, l + 1, n)
                        load_k(i, l + 1, n)
                    store_parts(i, l + 1, 0, 1)
                    load_maxima(i, l, 7)
                    scores_done(i, l, 6)
                    load_q(i, l + 1, 2)
                    load_k(i, l + 1, 2)
                    load_maxima(i, l, 8)
                    load_maxima(i, l, 9)
                    load_maxima(i, l, 10)
                    scores_done(i, l, 7)
                    load_q(i, l + 1, 3)
                    load_k(i, l + 1, 3)
                next_batch(i, 1)
            for c in range(CH):
                sp.wait_ge(stored[c], 1 + 16 * NB)
                sp.wait_ge(x_loaded[c], 16 * (NB + 1))

        @block.gpsimd
        def _(pool):
            link, enter_loop, leave_loop = own_chain(pool, pool_done, LAYERS * CH)

            def then(ins):
                link(0, ins)

            def deviations(i, l, c):
                ts = slice(c * HT, (c + 1) * HT)
                pool.wait_ge(stat_ready, at(i, l, CH, c + 1))
                apart(pool)
                link(i, pool.tensor_scalar(rstd[:, ts], mv[:, ts, 1], EPS, None, ALU.add))
                pool.tensor_tensor(rstd[:, ts], rstd[:, ts], half[:, 0:HT], ALU.pow).then_inc(rstd_ready, 1)

            def gate_rows(i, l, q):
                c, e, k = q // (E * KD), q // KD % E, q % KD
                n = c * E + e
                pool.wait_ge(wb_loaded[n % 4], at(i, l, 64, 16 * (n // 4 + 1)))
                pool.wait_ge(hs_used, at(i, l, QUANTA, q + 1))
                if l == 0:
                    pool.wait_ge(h_read, i * QUANTA + (q + 2))
                    src = hid[:, q % 2]
                else:
                    src = xnT[:, k, c * BANK:(c + 1) * BANK]
                pool.tensor_tensor(hs[:, (l * QUANTA + q) % 3], src, wb[:, n % 4], ALU.mult).then_inc(hs_ready, 1)

            def step(i, l, s):
                if s == LN1 + 1 and l >= 0:
                    deviations(i, l, 1)
                if s == LN0 + 1:
                    deviations(i, l + 1, 0)
                for r, q in begun(l, s):
                    gate_rows(i, r, q)
                if unit(l, s) is not None and is_diag(s):
                    pool.wait_ge(st_read, st_done(i, l, "unit", s, GH - 1))
                    apart(pool)
                    tri = probs[:, s % 2, :, 0:P]
                    pool.affine_select(out=tri, in_=tri, compare_op=ALU.is_ge, fill=0.0, base=0,
                                       pattern=[[0, GH], [1, P]], channel_multiplier=-1).then_inc(masked, 1)
                for c, n, r in projections(l, s - 1):
                    pool.wait_ge(mid_ready, at(i, r, CH * NP, c * NP + n + 1))
                    pool.tensor_tensor(parts[:, n // 2, n % 2, 2], rest[:, n % 2], parts[:, n // 2, n % 2, 1],
                                       ALU.subtract).then_inc(parts_ready, 1)

            pool.memset(half[:], -0.5).then_inc(parts_ready, 2)
            pool.memset(mask[:], 0.0).then_inc(hs_ready, 2)
            for m in (ident, identb):
                then(pool.memset(m[:], 0.0))
            pool.wait_ge(parts_ready, 2)
            then(pool.affine_select(out=ident[:], in_=ident[:], compare_op=ALU.not_equal, fill=1.0, base=0,
                                    pattern=[[-1, P]], channel_multiplier=1))
            pool.affine_select(out=identb[:], in_=identb[:], compare_op=ALU.not_equal, fill=1.0, base=0,
                               pattern=[[-1, P]], channel_multiplier=1).then_inc(consts, 1)
            for l, s in BEFORE[:2]:
                step(0, l, s)
            for m in (v, gateT, gate, earlier):
                then(pool.memset(m[:], 0.0))
            pool.wait_ge(hs_ready, 2)
            tri = mask[:, BANK - P:BANK]
            then(pool.affine_select(out=tri, in_=tri, compare_op=ALU.is_ge, fill=LOWEST, base=0,
                                    pattern=[[-1, P]], channel_multiplier=1))
            then(pool.affine_select(out=earlier[:], in_=earlier[:], compare_op=ALU.is_ge, fill=1.0, base=0,
                                    pattern=[[-1, E], [1, E]], channel_multiplier=0))
            ones = v[:, :, 0:H * VW].rearrange("p t (h d) -> p t h d", d=VW)[:, :, :, DH:VW]
            then(pool.memset(ones, 1.0))
            pool.memset(gate[:, :, E:E + 1], 1.0).then_inc(consts, 1)

            for l, s in BEFORE[2:]:
                step(0, l, s)
            enter_loop()
            with pool.Fori(0, NB) as i:
                for l, s in BODY:
                    step(i, l, s)
            leave_loop()

        @block.scalar
        def _(act):
            act.wait_ge(consts, 1)
            for col, (s, n) in enumerate(((st_read, 2), (h_read, 1), (o_read, 1))):
                act.activation(graw[:, 0, col:col + 1], half[:, 0:1], ACT.Exp).then_inc(s, n)
            load = lambda dst, src, s: act.dma_start(dst, src).then_inc(s, 16)
            for dst, src in ((w1, A["w1"]), (w2, A["w2"])):
                load(dst[:], src.rearrange("e (k p) n -> p e k n", p=P), w_moe[0])
            load(b1[:], A["b1"], w_moe[0])
            load(wqk[1][:, 0], A["wk"][1].rearrange("(k p) n -> p k n", p=P), w_attn[1])
            load(wqk[1][:, 1], A["wq"][1].rearrange("(k p) n -> p k n", p=P), w_attn[1])
            load(wvg[1][:], A["wvg"][1].rearrange("(k p) n -> p k n", p=P), w_attn[1])
            load(wo[1][:], A["wo"][1].rearrange("(k p) n -> p k n", p=P), w_attn[1])
            load(wbias[1][:], A["wbias"][1], w_attn[1])
            load(bg[1][:], A["bg"][1].partition_broadcast(P), w_attn[1])
            load(we[:], A["we"].rearrange("e (k p) n -> p e k n", p=P), w_moe[1])

            def full(i, *key):
                act.wait_ge(st_full, st_no(i, *key) + 1)
                return pst[ST[key] % 2]

            def exponentials(i, l, s, j):
                w = unit_cols(s)[1]
                if j == 0:
                    act.wait_ge(probs_used, at(i, l, NU, s + 1))
                ps = full(i, l, "unit", s, j)
                act.activation(probs[:, s % 2, j, 0:w], ps[:, 0:w], ACT.Exp, scale=DH ** -0.5).then_inc(st_read, 1)

            def hidden(i, l, p):
                if l == 0 and p % 2 == 1 and p < 2 * QUANTA:
                    q = p // 2
                    act.wait_ge(h_full, i * QUANTA + (q + 1))
                    act.wait_ge(hs_ready, at(i, 0, QUANTA, q + 1))
                    act.wait_ge(w_moe[0], 48)
                    act.activation(hid[:, q % 2], ph[:], ACT.Relu,
                                   bias=b1[:, q // KD % E, q % KD:q % KD + 1]).then_inc(h_read, 1)

            def spread_gates(i, l, n):
                c = n // E
                if n % E == 0:
                    act.wait_ge(gate_stored[c], at(i, l, 16, 16))
                last = 2 * (n - 4) + 2 if n >= 4 else 0
                act.wait_ge(hs_ready, at(i, l, QUANTA, 2 + last))
                apart(act)
                act.dma_start(wb[:, n % 4], gate_dram[c, n % E].partition_broadcast(P)
                              ).then_inc(wb_loaded[n % 4], 16)

            spread_at = {}
            for l in range(LAYERS):
                for n in range(CH * E):
                    free = 0
                    if n >= 4:
                        free = next(s for s in range(NU) if (l, 2 * (n - 4) + 1) in begun(l, s))
                    spread_at.setdefault((l, max(free, WB_FIRST[n // E]) + (n % E if n < 4 else 0) // 2), []).append(n)

            def step(i, l, s):
                work = halves(l, s)
                for r, p in work[:1]:
                    hidden(i, r, p)
                if unit(l, s) is not None:
                    exponentials(i, l, s, 0)
                if l == 1 and s in GATES:
                    c = GATES.index(s)
                    act.wait_ge(logits_ready, i * CH + (c + 1))
                    act.activation(graw[:, c * HT:(c + 1) * HT], gs[:, c * HT:(c + 1) * HT],
                                   ACT.Exp).then_inc(gexp_ready, 1)
                for r, d in now(l, s):
                    n = ends_set(d - 1)
                    if r >= 0 and n is not None:
                        act.wait_ge(probs_used, at(i, r, NU, 2 + d))
                        act.activation(oraw[:], po[:], ACT.Copy).then_inc(o_read, 1)
                if unit(l, s) is not None:
                    exponentials(i, l, s, 1)
                for r, p in work[1:]:
                    hidden(i, r, p)
                if unit(l, s) is not None:
                    exponentials(i, l, s, 2)
                if unit(l, s) is not None:
                    exponentials(i, l, s, 3)
                for c, n, r in projections(l, s - 1):
                    act.wait_ge(mx_read, mx_done(i, l, "proj", c, n))
                    act.activation(parts[:, n // 2, n % 2, 1], rest[:, n % 2], ACT.Copy).then_inc(mid_ready, 1)
                for r, d in now(l, s):
                    for c, at_step in enumerate((OT0, OT1)):
                        if r >= 0 and d == at_step:
                            if (r, c) in ((0, 0), (1, 1)):
                                act.wait_ge(stored[1 - c], i * 16 + (1 + 16 * c))
                            for k in range(KD):
                                ps = full(i, r, "oT", c, k)
                                act.activation(attn[:, k], ps[:], ACT.Copy).then_inc(st_read, 1)
                    for c, at_step in enumerate((XT0, XT1)):
                        if d == at_step and (r >= 0 or c == 0):
                            for k in range(KD):
                                ps = full(i, r, "xT", c, k)
                                act.activation(xnT[:, k, c * BANK:(c + 1) * BANK], ps[:],
                                               ACT.Copy).then_inc(st_read, 1)
                    for c, n, r1 in projections(r, d):
                        if (r, c) != (-1, 0):
                            act.wait_ge(qk_stored[n // 2], at(i, r1, CH * 32, c * 32))
                        act.wait_ge(mx_full, mx_no(i, r, "proj", c, n) + 1)
                        act.activation(parts[:, n // 2, n % 2, 0], pmx[MX[r, "proj", c, n] % 2][:],
                                       ACT.Copy).then_inc(hi_ready, 1)
                    for t, _ in value_tiles(r, d):
                        if l < 0:
                            act.wait_ge(consts, 2)
                        ps = full(i, r, "v", t)
                        dst = v[:, t, 0:H * VW].rearrange("p (h d) -> p h d", d=VW)[:, :, 0:DH]
                        act.activation(dst, ps[:, 0:D].rearrange("p (h d) -> p h d", d=DH), ACT.Copy)
                        act.activation(graw[:, t], ps[:, D:D + E], ACT.Copy).then_inc(st_read, 1)
                for n in spread_at.get((l, s), []):
                    spread_gates(i, l, n)

            for l, s in BEFORE:
                step(0, l, s)
            with act.Fori(0, NB) as i:
                for l, s in BODY:
                    step(i, l, s)

        @block.vector
        def _(dve):
            for col, (s, n) in enumerate(((mx_read, 2), (y_read, 2))):
                dve.memset(junk[:, col:col + 1], 0.0).then_inc(s, n)

            link, enter_loop, leave_loop = own_chain(dve, dve_done, LAYERS * (CH + 5 * CH + 5 * NSETS) + 7 * CH)

            def full(i, *key):
                dve.wait_ge(mx_full, mx_no(i, *key) + 1)
                return pmx[MX[key] % 2]

            def statistics(i, c):
                for t in range(c * HT, (c + 1) * HT):
                    ins = dve.bn_stats(stats[:, t], x[:, t])
                link(i, ins)
                for t in range(c * HT, (c + 1) * HT):
                    ins = dve.bn_aggr(mv[:, t], stats[:, t])
                ins.then_inc(stat_ready, 1)

            def normalise(i, l, c):
                dve.wait_ge(rstd_ready, at(i, l, CH, c + 1))
                for t in range(c * HT, (c + 1) * HT):
                    dve.tensor_scalar(xn[:, t - c * HT], x[:, t], mv[:, t, 0:1], rstd[:, t:t + 1], ALU.subtract,
                                      ALU.mult).then_inc(xn_ready, 1)

            def maximum(i, l, n, k):
                j, t, a, b = pieces_of(n)[k]
                col = j * HT + t % HT
                if k == 0 and (l, n) not in ((-1, NSETS), (-1, NSETS + 1)):
                    dve.wait_ge(msplit_ready, at(i, l, NSETS, n - 1))
                    apart(dve)
                src = full(i, l, "max", n, k)[:, 0:b - a]
                if b < (t + 1) * P:
                    dve.tensor_reduce(rmax0[:, col:col + 1], src, AX_X, ALU.max).then_inc(mx_read, 1)
                else:
                    apart(dve)
                    if a:
                        dve.wait_ge(mx_read, mx_done(i, l, "max", n, k - GH * HT))
                        apart(dve)
                    dve.tensor_tensor_reduce(
                        out=src, in0=src, in1=mask[:, BANK - (b - a):BANK], op0=ALU.add,
                        op1=ALU.max, scale=1.0, scalar=rmax0[:, col:col + 1] if a else LOWEST,
                        accum_out=rmax[:, n % 2, col:col + 1]).then_inc(mx_read, 1)

            def gates(i, l, c, part):
                ts = slice(c * HT, (c + 1) * HT)
                tile_e = lambda a: a[:, ts].unsqueeze(2).broadcast_to([P, HT, E])
                value, picked = gs[:, ts], gate[:, ts, 0:E]
                other = value.unsqueeze(2).broadcast_to([P, HT, E, E])
                own = value.unsqueeze(3).broadcast_to([P, HT, E, E])
                if part == 0:
                    if c == 0:
                        dve.wait_ge(st_read, i * NST + (BEGIN[l][1] + 2))
                    else:
                        dve.wait_ge(st_read, st_done(i, l, "v", NT - 1))
                    dve.wait_ge(w_attn[l], 96)
                    link(i, dve.tensor_tensor(value, graw[:, ts], bg[l][:].unsqueeze(1).broadcast_to([P, HT, E]),
                                              ALU.add))
                elif part == 1 and l == 1:
                    link(i, dve.tensor_reduce(gtot[:, ts], value, AX_X, ALU.max))
                elif part == 2 and l == 1:
                    dve.tensor_tensor(value, value, tile_e(gtot), ALU.subtract).then_inc(logits_ready, 1)
                elif part == 3 and l == 1:
                    dve.wait_ge(gexp_ready, i * CH + (c + 1))
                    link(i, dve.tensor_reduce(gtot[:, ts], graw[:, ts], AX_X, ALU.add))
                elif part == 4 and l == 1:
                    link(i, dve.reciprocal(ginv[:, ts], gtot[:, ts]))
                elif part == 5 and l == 1:
                    link(i, dve.tensor_tensor(value, graw[:, ts], tile_e(ginv), ALU.mult))
                elif part == 6:
                    dve.tensor_tensor(cgt[:], other, own, ALU.is_gt)
                elif part == 7:
                    link(i, dve.tensor_tensor(cge[:], other, own, ALU.is_ge))
                elif part == 8:
                    link(i, dve.tensor_tensor(cge[:], cge[:], earlier[:].unsqueeze(1).broadcast_to([P, HT, E, E]),
                                              ALU.mult))
                elif part == 9:
                    link(i, dve.tensor_tensor(cgt[:], cgt[:], cge[:], ALU.max))
                elif part == 10:
                    link(i, dve.tensor_reduce(rank[:, ts], cgt[:], AX_X, ALU.add))
                elif part == 11:
                    pick = dve.scalar_tensor_tensor(out=picked, in0=rank[:, ts], scalar=1.5, in1=value,
                                                    op0=ALU.is_lt, op1=ALU.mult)
                    if l == 1:
                        link(i, pick)
                        link(i, dve.tensor_reduce(gtot[:, ts], picked, AX_X, ALU.add))
                    else:
                        pick.then_inc(gate_ready, 1)
                elif part == 12 and l == 1:
                    link(i, dve.reciprocal(ginv[:, ts], gtot[:, ts]))
                    dve.tensor_tensor(picked, picked, tile_e(ginv), ALU.mult).then_inc(gate_ready, 1)

            def attention_output(i, l, n):
                g, c = n % NG, n // NG
                if n == NG:
                    dve.wait_ge(st_full, st_no(i, l, "oT", 0, KD - 1) + 1)
                src = full(i, l, "out", n)[:].rearrange("p (t h d) -> p t h d", h=GH, d=HS)
                total = osum[:, n % 2]
                link(i, dve.tensor_scalar(total, src[:, :, :, DH], TINY, None, ALU.max))
                link(i, dve.reciprocal(total, total))
                dst = otok[:, :, g * GH * DH:(g + 1) * GH * DH]
                dve.tensor_tensor(dst.rearrange("p t (h d) -> p t h d", d=DH), src[:, :, :, 0:DH],
                                  total.unsqueeze(3).broadcast_to([P, HT, GH, DH]),
                                  ALU.mult).then_inc(mx_read, 1)

            def add_attention(i, l, c):
                dve.wait_ge(y_read, at(i, l, NY, 2 + 2 * (c + 1)))
                if l == LAYERS - 1:
                    dve.wait_ge(mx_full, mx_no(i, l, "y", 2 * c + 1) + 1)
                for b in range(2 * c, 2 * c + 2):
                    ps = full(i, l, "y", b)
                    rows = slice(2 * b, 2 * b + 2)
                    dst = x[:, rows] if l == 0 else result[:, 2 * b - c * HT:2 * b - c * HT + 2]
                    dve.tensor_tensor(dst.rearrange("p t d -> p (t d)"), ps[:],
                                      x[:, rows].rearrange("p t d -> p (t d)"), ALU.add).then_inc(mx_read, 1)

            def add_experts(i, l, c, b):
                dve.wait_ge(hs_used, at(i, l, QUANTA, 3 + (c + 1) * E * KD))
                t = c * HT + b * 2
                dve.tensor_tensor(x[:, t:t + 2].rearrange("p t d -> p (t d)"), py[b][:],
                                  x[:, t:t + 2].rearrange("p t d -> p (t d)"), ALU.add).then_inc(y_read, 1)

            def split_maxima(i, l, n):
                dve.wait_ge(mx_read, mx_done(i, l, "max", n, len(pieces_of(n)) - 1))
                apart(dve)
                m = GH * HT
                link(i, dve.tensor_scalar(mrest[:], rmax[:, n % 2], -1.0, None, ALU.mult))
                link(i, dve.tensor_copy(mparts[:, 0:m], mrest[:]))
                link(i, dve.tensor_tensor(mrest[:], mrest[:], mparts[:, 0:m], ALU.subtract))
                dve.tensor_copy(mparts[:, m:2 * m], mrest[:]).then_inc(msplit_ready, 1)

            def turn_maxima(i, l, n):
                ps = full(i, l, "turn", n)
                if (l, n) != (-1, NSETS):
                    dve.wait_ge(mrow_loaded, at(i, l, NSETS * 32, 32 * n))
                dve.tensor_copy(mT[:], ps[:].bitcast(BF16)[0:MROWS * GH * HT, 0:P]).then_inc(mx_read, 1)

            def step(i, l, s):
                work = bundle(l, s)
                if turned(l, s) is not None:
                    split_maxima(i, l, turned(l, s))
                for m in range(max(len(work), 4)):
                    if m == before_turn(l, s) and turned(l, s) is not None:
                        turn_maxima(i, l, turned(l, s))
                    for n, k in work[m:m + 1]:
                        maximum(i, l, n, k)
                    if m == 0:
                        for r, c in experts_done(l, s - 1):
                            add_experts(i, r, c, 1)
                    if m == 2 and s == LN0 + 1:
                        normalise(i, l + 1, 0)
                    if m == 2 and s == LN1 + 1 and l >= 0:
                        normalise(i, l, 1)
                    for c, first in enumerate(GATES):
                        part = ((s - first) * 4 + m) * GATE_PACE[c]
                        if l >= 0 and s >= first and m < 4:
                            for n in range(part, min(part + GATE_PACE[c], GATE_PARTS)):
                                gates(i, l, c, n)
                for r, c in experts_done(l, s):
                    add_experts(i, r, c, 0)
                for r, d in now(l, s):
                    if r >= 0 and ends_set(d - 2) is not None:
                        attention_output(i, r, ends_set(d - 2))
                    for c, at_step in enumerate((Y0, Y1)):
                        if r >= 0 and d == at_step:
                            add_attention(i, r, c)
                    if r >= 0 and d in GATE_ROWS:
                        c = GATE_ROWS.index(d)
                        ps = full(i, r, "gateT", c)
                        dve.tensor_copy(gateT[0:GR, c * BANK:(c + 1) * BANK], ps[0:GR, :]).then_inc(mx_read, 1)
                    for c, n, r1 in projections(r, d):
                        p = c * NP + n
                        dve.wait_ge(hi_ready, at(i, r1, CH * NP, p + 1))
                        dve.wait_ge(parts_ready, at(i, r1, CH * NP, p + 1))
                        dve.tensor_tensor(rest[:, n % 2], pmx[MX[r, "proj", c, n] % 2][:],
                                          parts[:, n // 2, n % 2, 0], ALU.subtract).then_inc(mx_read, 1)
                if s == LN0:
                    if l == 0:
                        dve.wait_ge(mx_read, mx_done(i, l, "y", 1))
                    else:
                        dve.wait_ge(x_loaded[0], i * 16 + (16 if l < 0 else 32))
                    apart(dve)
                    statistics(i, 0)
                if s == LN1 and l >= 0:
                    if l == 0:
                        dve.wait_ge(x_loaded[1], i * 16 + 16)
                    else:
                        dve.wait_ge(mx_read, mx_done(i, 0, "y", 3))
                    apart(dve)
                    statistics(i, 1)

            for l, s in BEFORE:
                if s == XT0 + 1:
                    dve.memset(k_first[STACK:P], 1.0)
                    dve.memset(k_second[STACK:P], 1.0)
                    dve.wait_ge(consts, 2)
                step(0, l, s)
            enter_loop()
            with dve.Fori(0, NB) as i:
                for l, s in BODY:
                    step(i, l, s)
            leave_loop()

        @block.tensor
        def _(pe):
            pe.wait_ge(consts, 1)
            for b, (s, n) in enumerate(((probs_used, 2), (hs_used, 3))):
                pe.transpose(py[b][:, 0:P], ident[:], ident[:]).then_inc(s, n)

            def mx(i, *key):
                pe.wait_ge(mx_read, mx_no(i, *key) + 1)
                return pmx[MX[key] % 2]

            def st(i, *key):
                pe.wait_ge(st_read, st_no(i, *key) + 1)
                return pst[ST[key] % 2]

            def scores(i, l, s, j):
                if unit(l, s) is None:
                    return
                n, k = UNITS[s]
                a, w = unit_cols(s)
                a %= BANK
                if j == 0 and k == 0:
                    pe.wait_ge(mrow_loaded, at(i, l, NSETS * 32, 32 * (n + 1)))
                ps = st(i, l, "unit", s, j)
                keys = k_first[:, n % NG] if k < HT else k_second[:, n % 2]
                pe.matmul(ps[:, 0:w], keys[0:SROWS, j, k % HT * P:(k % HT + 1) * P],
                          qs[0:SROWS, n % NG, j, a:a + w], start=True, stop=True).then_inc(st_full, 1)

            def maxima(i, l, s, m):
                ps = bundle(l, s)
                if m not in PLACES[len(ps)]:
                    return
                n, k = ps[PLACES[len(ps)].index(m)]
                j, t, a, b = pieces_of(n)[k]
                if k == 0:
                    pe.wait_ge(q_loaded[n % NG], at(i, l, 2 * 96, (n // NG + 1) * 96))
                    if n % NSETS < NG:
                        pe.wait_ge(k_first_loaded[n % NG], at(i, l, 96, (n // NSETS + 1) * 96))
                if k == GH * HT:
                    pe.wait_ge(k_second_loaded[n % 2], at(i, l, 2 * 96, (n % NG // 2 + 1) * 96))
                bk = mx(i, l, "max", n, k)
                keys = k_first[:, n % NG] if a == 0 else k_second[:, n % 2]
                pe.matmul(bk[:, 0:b - a], qs[0:STACK, n % NG, j, t % HT * P:(t % HT + 1) * P],
                          keys[0:STACK, j, 0:b - a], start=True, stop=True).then_inc(mx_full, 1)

            def hidden(i, l, p):
                if l == 0 and p < 2 * QUANTA:
                    q, k = p // 2, p % 2
                    c, e, m = q // (E * KD), q // KD % E, q % KD
                    if k == 0:
                        pe.wait_ge(w_moe[0], 48)
                        pe.wait_ge(h_read, i * QUANTA + (q + 1))
                    mm = pe.matmul(ph[:], w1[:, e, k, m * P:(m + 1) * P],
                                   xnT[:, k, c * BANK:(c + 1) * BANK], start=(k == 0), stop=(k == KD - 1))
                    if k == KD - 1:
                        mm.then_inc(h_full, 1)

            def expert_out(i, l, p, m):
                if p < LAG:
                    return
                q, t = (p - LAG) // 2, (p - LAG) % 2 * 2 + m
                e, k = q // KD % E, q % KD
                c = q // (E * KD)
                first, last = q % (E * KD) == 0, q % (E * KD) == E * KD - 1
                if t == 0:
                    pe.wait_ge(w_moe[l], 48 if l == 0 else 16)
                    pe.wait_ge(hs_ready, at(i, l, QUANTA, 2 + q + 1))
                if first and t % 2 == 0:
                    pe.wait_ge(y_read, at(i, l, NY, 2 * c + t // 2 + 1))
                mm = pe.matmul(py[t // 2][:, t % 2 * D:(t % 2 + 1) * D],
                               hs[:, (l * QUANTA + q) % 3, t * P:(t + 1) * P], (w2 if l == 0 else we)[:, e, k],
                               start=first and t % 2 == 0, stop=last, skip_group_check=True)
                if t == HT - 1:
                    mm.then_inc(hs_used, 1)

            def attend(i, l, s):
                for r, d in now(l, s):
                    if r < 0 or not 1 <= d <= NU:
                        continue
                    u = d - 1
                    n, k = UNITS[u]
                    g = n % NG
                    w = unit_cols(u)[1]
                    if is_diag(u):
                        pe.wait_ge(masked, at(i, r, NDIAG, DIAG_NO[u] + 1))
                    else:
                        pe.wait_ge(st_read, st_done(i, r, "unit", u, GH - 1))
                    if k == 0:
                        pe.wait_ge(o_read, at(i, r, NSETS, n + 1))
                    for j in range(GH):
                        col = (GH * g + j) * VW
                        mm = pe.matmul(po[HS * j:HS * (j + 1), BANK - w:BANK], v[:, k, col:col + HS],
                                       probs[:, u % 2, j, 0:w], start=(k == 0), stop=ends_set(u) is not None)
                    mm.then_inc(probs_used, 1)

            def turn(i, ps, src, k):
                for t in range(HT):
                    mm = pe.transpose(ps[:, t * P:(t + 1) * P], src[:, t, k * P:(k + 1) * P], ident[:])
                mm.then_inc(st_full, 1)

            def turn_maxima(i, l, n):
                pe.wait_ge(msplit_ready, at(i, l, NSETS, n + 1))
                bk = mx(i, l, "turn", n)
                apart(pe)
                pe.transpose(bk[:].bitcast(BF16)[0:MROWS * GH * HT, 0:P], mparts[:], identb[:]).then_inc(mx_full, 1)

            def turn_set(i, l, n):
                pe.wait_ge(o_read, at(i, l, NSETS, 1 + n + 1))
                bk = mx(i, l, "out", n)
                for t in range(HT):
                    mm = pe.transpose(bk[:, t * P:(t + 1) * P], oraw[:, t * P:(t + 1) * P], ident[:])
                mm.then_inc(mx_full, 1)

            def turn_output(i, l, c):
                pe.wait_ge(mx_read, mx_done(i, l, "out", (c + 1) * NG - 1))
                for k in range(KD):
                    turn(i, st(i, l, "oT", c, k), otok, k)

            def project_output(i, l, c):
                pe.wait_ge(st_read, st_done(i, l, "oT", c, KD - 1))
                for b in range(2 * c, 2 * c + 2):
                    ps = mx(i, l, "y", b)
                    for t in range(2):
                        tile = 2 * b + t
                        local = tile - c * HT
                        pe.matmul(ps[:, t * D:(t + 1) * D], gateT[:, tile * P:(tile + 1) * P], wbias[l][:],
                                  start=(t == 0), stop=False, skip_group_check=True)
                        for k in range(KD):
                            mm = pe.matmul(ps[:, t * D:(t + 1) * D], attn[:, k, local * P:(local + 1) * P],
                                           wo[l][:, k], start=False, stop=(k == KD - 1), skip_group_check=True)
                    mm.then_inc(mx_full, 1)

            def turn_gates(i, l, c):
                pe.wait_ge(gate_ready, at(i, l, CH, c + 1))
                ps = mx(i, l, "gateT", c)
                for t in range(HT):
                    mm = pe.transpose(ps[0:GR, t * P:(t + 1) * P], gate[:, HT * c + t], ident[:])
                mm.then_inc(mx_full, 1)

            def project(i, l, c, n, r):
                pe.wait_ge(w_attn[r % LAYERS], 96)
                pe.wait_ge(st_read, st_done(i, l, "xT", c, KD - 1))
                ps = mx(i, l, "proj", c, n)
                tile, q = n // 2, n % 2
                for k in range(KD):
                    mm = pe.matmul(ps[:], wqk[r % LAYERS][:, q, k, tile * P:(tile + 1) * P],
                                   xnT[:, k, c * BANK:(c + 1) * BANK], start=(k == 0), stop=(k == KD - 1))
                mm.then_inc(mx_full, 1)

            def values(i, l, t, r):
                ps = st(i, l, "v", t)
                for k in range(KD):
                    mm = pe.matmul(ps[:, 0:D + E], xnT[:, k, t * P:(t + 1) * P], wvg[r % LAYERS][:, k],
                                   start=(k == 0), stop=(k == KD - 1))
                mm.then_inc(st_full, 1)

            def step(i, l, s):
                one, two = halves(l, s)[:1], halves(l, s)[1:]
                for r, p in one:
                    hidden(i, r, p)
                    if r == 1:
                        expert_out(i, r, p, 0)
                maxima(i, l, s, 0)
                scores(i, l, s, 0)
                maxima(i, l, s, 1)
                if attends_late(l, s):
                    maxima(i, l, s, 2)
                    scores(i, l, s, 1)
                attend(i, l, s)
                if turned(l, s) is not None:
                    turn_maxima(i, l, turned(l, s))
                if not attends_late(l, s):
                    maxima(i, l, s, 2)
                    scores(i, l, s, 1)
                for r, p in two:
                    hidden(i, r, p)
                    if r == 1:
                        expert_out(i, r, p, 0)
                maxima(i, l, s, 3)
                for r, p in one:
                    expert_out(i, r, p, 1 if r == 1 else 0)
                maxima(i, l, s, 4)
                scores(i, l, s, 2)
                for r, p in one:
                    if r == 0:
                        expert_out(i, r, p, 1)
                if l == 1:
                    scores(i, l, s, 3)
                maxima(i, l, s, 5)
                for r, p in two:
                    expert_out(i, r, p, 1 if r == 1 else 0)
                if l != 1:
                    scores(i, l, s, 3)
                for r, p in two:
                    if r == 0:
                        expert_out(i, r, p, 1)
                maxima(i, l, s, 6)
                for r, d in now(l, s):
                    if r >= 0 and ends_set(d - 2) is not None:
                        turn_set(i, r, ends_set(d - 2))
                    for c, at_step in enumerate((OT0, OT1)):
                        if r >= 0 and d == at_step:
                            turn_output(i, r, c)
                    for c, at_step in enumerate((Y0, Y1)):
                        if r >= 0 and d == at_step:
                            project_output(i, r, c)
                    if r >= 0 and d in GATE_ROWS:
                        turn_gates(i, r, GATE_ROWS.index(d))
                    for c, at_step in enumerate((XT0, XT1)):
                        if d == at_step and (r >= 0 or c == 0):
                            pe.wait_ge(xn_ready, at(i, r + 1 - c, NT, (c + 1) * HT))
                            for k in range(KD):
                                turn(i, st(i, r, "xT", c, k), xn, k)
                    for c, n, r1 in projections(r, d):
                        project(i, r, c, n, r1)
                    for t, r1 in value_tiles(r, d):
                        values(i, r, t, r1)

            for l, s in BEFORE:
                step(0, l, s)
            with pe.Fori(0, NB) as i:
                for l, s in BODY:
                    step(i, l, s)


def kernel(**inputs):
    import numpy as np
    import concourse.bacc as bacc
    from concourse.bass_utils import run_bass_kernel_spmd

    g = {k: np.asarray(a) for k, a in inputs.items()}

    def biases(expert_bias, out_bias):
        rows = np.zeros((P, D), expert_bias.dtype)
        rows[:E] = expert_bias
        if out_bias is not None:
            rows[E] = out_bias
        return rows

    per_layer = {
        "wk": [g["L0_attn_Wk"].T, g["L1_attn_Wk"].T],
        "wq": [g["L0_attn_Wq"].T, g["L1_attn_Wq"].T],
        "wvg": [np.concatenate([g["L0_attn_Wv"].T, g["L0_ffn_W_gate"]], 1),
                np.concatenate([g["L1_attn_Wv"].T, g["L1_ffn_Wg"]], 1)],
        "wo": [g["L0_attn_Wo"].T, g["L1_attn_Wo"].T],
        "wbias": [biases(g["L0_ffn_b2"], None), biases(g["L1_ffn_be"], g["L1_attn_bo"])],
        "bg": [g["L0_ffn_b_gate"], g["L1_ffn_bg"]],
    }
    data = {"x": g["L0_attn_x"], "w1": g["L0_ffn_W1"], "w2": g["L0_ffn_W2"], "b1": g["L0_ffn_b1"].reshape(E, KD, P).transpose(2, 0, 1),
            "we": g["L1_ffn_We"]}
    nc = bacc.Bacc("TRN2", target_bir_lowering=False, num_devices=1)
    arrays, A = {}, {}

    def declare(name, a):
        a = np.ascontiguousarray(a)
        arrays[f"in_{name}"] = a
        return nc.dram_tensor(f"in_{name}", a.shape, mybir.dt.from_np(a.dtype), kind="ExternalInput").ap()

    for name, a in data.items():
        A[name] = declare(name, a)
    for name, both in per_layer.items():
        A[name] = [declare(f"{name}{l}", a) for l, a in enumerate(both)]
    out = nc.dram_tensor("out_0", (NB, T, D), F32, kind="ExternalOutput").ap()
    attention_moe_kernel(nc, A, out)
    r = run_bass_kernel_spmd(nc, [arrays], core_ids=[0])
    return r.results[0]["out_0"]
```
